# Optimizing a Trainium2 kernel written in Bass

```python
import numpy as np
import jax
import jax.numpy as jnp

def _softmax(x, axis=-1):
    return jax.nn.softmax(x, axis=axis)

def _gelu(x):
    return jax.nn.gelu(x, approximate=True)

def _silu(x):
    return jax.nn.silu(x)

def _sigmoid(x):
    return jax.nn.sigmoid(x)

def _layernorm(x, axis=-1, eps=1e-05):
    m = jnp.mean(x, axis=axis, keepdims=True)
    v = jnp.var(x, axis=axis, keepdims=True)
    return (x - m) / jnp.sqrt(v + eps)

def _scatter_add(tgt, idx, src, axis=0):
    return tgt.at[idx].add(src)

def _segment_sum(src, seg, n):
    return jax.ops.segment_sum(src, seg, n)
kernel_name = 'mk_gnn_resnorm_d4_gnn_r8_66ef4c'

def setup_inputs(seed: int=0):
    np.random.seed(seed)
    _w = jnp.asarray

    def _rec_inputs():
        import jax
        import jax.numpy as jnp
        _gk = jax.random.key(seed)
        x = -8.776e-05 + 1 * jax.random.normal(jax.random.fold_in(_gk, 1), (6250, 128), jnp.float32)
        src = jax.random.randint(jax.random.fold_in(_gk, 2), (100000,), 0, 6250, jnp.int32)
        dst = jax.random.randint(jax.random.fold_in(_gk, 3), (100000,), 0, 6250, jnp.int32)
        _o = jnp.argsort(dst, stable=True)
        src = src[_o]
        dst = dst[_o]
        edge_type_32 = jax.random.randint(jax.random.fold_in(_gk, 13), (100000,), 0, 32, jnp.int32)
        edge_weight = jax.random.uniform(jax.random.fold_in(_gk, 14), (100000,), jnp.float32, 0.0, 0.999998)
        return (x, src, dst, edge_type_32, edge_weight)
    x, src, dst, edge_type_32, edge_weight = _rec_inputs()

    def _L0_gnn_setup():
        import jax, jax.numpy as jnp
        import numpy as np
        N = 5000
        E = 80000
        IN = 128
        H = 4
        C = 32
        key = jax.random.key(seed)
        ks = jax.random.split(key, 5)
        x = jax.random.normal(ks[0], (N, IN), dtype=jnp.float32)
        edge_index = jax.random.randint(ks[1], (2, E), 0, N, dtype=jnp.int64)
        W_lin = jax.random.normal(ks[2], (IN, H * C), dtype=jnp.float32) * 0.05
        b_lin = jnp.zeros((H * C,), dtype=jnp.float32)
        W_att = jax.random.normal(ks[3], (2 * H * C, H), dtype=jnp.float32) * 0.05
        b_att = jnp.zeros((H,), dtype=jnp.float32)
        return {'x': x, 'edge_index': edge_index, 'W_lin': W_lin, 'b_lin': b_lin, 'W_att': W_att, 'b_att': b_att}
    _L0_gnn_all = _L0_gnn_setup()
    _L0_gnn_in = {k: v for k, v in _L0_gnn_all.items() if k in ('W_lin', 'b_lin', 'W_att', 'b_att')}
    del _L0_gnn_all

    def _L1_gnn_setup():
        import jax, jax.numpy as jnp
        import numpy as np
        EPS = 0.0
        key = jax.random.key(seed)
        kx, ke, kw, k1, k2 = jax.random.split(key, 5)
        N, E, D, H = (12500, 75000, 128, 128)
        x = jax.random.normal(kx, (N, D), dtype=jnp.float32)
        edge_index = jax.random.randint(ke, (2, E), 0, N, dtype=jnp.int64)
        edge_weight = jax.random.uniform(kw, (E,), dtype=jnp.float32)
        W1 = jax.random.normal(k1, (D, H), dtype=jnp.float32) * (1.0 / np.sqrt(D))
        b1 = jnp.zeros((H,), dtype=jnp.float32)
        W2 = jax.random.normal(k2, (H, D), dtype=jnp.float32) * (1.0 / np.sqrt(H))
        b2 = jnp.zeros((D,), dtype=jnp.float32)
        return {'x': x, 'edge_index': edge_index, 'edge_weight': edge_weight, 'W1': W1, 'b1': b1, 'W2': W2, 'b2': b2}
    _L1_gnn_all = _L1_gnn_setup()
    _L1_gnn_in = {k: v for k, v in _L1_gnn_all.items() if k in ('W1', 'b1', 'W2', 'b2')}
    del _L1_gnn_all

    def _L2_gnn_setup():
        import jax, jax.numpy as jnp
        import numpy as np
        N = 3750
        E = 120000
        DIN = 128
        DOUT = 128
        R = 32
        NUM_RULES = 100
        ACTIVE = 4
        EPS = 1e-05
        key = jax.random.key(seed)
        ks = jax.random.split(key, 10)
        x = jax.random.normal(ks[0], (N, DIN), jnp.float32)
        src = jax.random.randint(ks[1], (E,), 0, N)
        dst = jax.random.randint(ks[2], (E,), 0, N)
        edge_type = jax.random.randint(ks[3], (E,), 0, R)
        rule_ids = jax.random.randint(ks[4], (ACTIVE,), 0, NUM_RULES)
        W_r = jax.random.normal(ks[5], (R, DIN, DOUT), jnp.float32) * 0.05
        Wq_w = jax.random.normal(ks[6], (DIN, DOUT), jnp.float32) * 0.05
        Wq_b = jnp.zeros((DOUT,), jnp.float32)
        Wk_w = jax.random.normal(ks[7], (3 * DIN, DOUT), jnp.float32) * 0.05
        Wk_b = jnp.zeros((DOUT,), jnp.float32)
        rule_emb = jax.random.normal(ks[8], (NUM_RULES, DIN), jnp.float32) * 0.05
        bias = jnp.zeros((DOUT,), jnp.float32)
        ln_gamma = jnp.ones((DOUT,), jnp.float32)
        ln_beta = jnp.zeros((DOUT,), jnp.float32)
        return {'x': x, 'W_r': W_r, 'Wq_w': Wq_w, 'Wq_b': Wq_b, 'Wk_w': Wk_w, 'Wk_b': Wk_b, 'rule_emb': rule_emb, 'bias': bias, 'ln_gamma': ln_gamma, 'ln_beta': ln_beta, 'src': src, 'dst': dst, 'edge_type': edge_type, 'rule_ids': rule_ids}
    _L2_gnn_all = _L2_gnn_setup()
    _L2_gnn_in = {k: v for k, v in _L2_gnn_all.items() if k in ('W_r', 'Wq_w', 'Wq_b', 'Wk_w', 'Wk_b', 'rule_emb', 'bias', 'ln_gamma', 'ln_beta', 'rule_ids')}
    del _L2_gnn_all

    def _L3_gnn_setup():
        import jax, jax.numpy as jnp
        import numpy as np
        N = 12500
        E = 200000
        D_IN = 128
        D_OUT = 128
        NEG_SLOPE = 0.2
        ALPHA = 0.2
        key = jax.random.key(seed)
        k1, k2, k3, k4, k5 = jax.random.split(key, 5)
        x = jax.random.normal(k1, (N, D_IN), dtype=jnp.float32)
        edge_index = jax.random.randint(k2, (2, E), 0, N, dtype=jnp.int64)
        W = jax.random.normal(k3, (D_IN, D_OUT), dtype=jnp.float32) / np.sqrt(D_IN)
        a_src = jax.random.normal(k4, (D_OUT,), dtype=jnp.float32) / np.sqrt(D_OUT)
        a_dst = jax.random.normal(k5, (D_OUT,), dtype=jnp.float32) / np.sqrt(D_OUT)
        bias = jnp.zeros((D_OUT,), dtype=jnp.float32)
        return {'x': x, 'edge_index': edge_index, 'W': W, 'a_src': a_src, 'a_dst': a_dst, 'bias': bias}
    _L3_gnn_all = _L3_gnn_setup()
    _L3_gnn_in = {k: v for k, v in _L3_gnn_all.items() if k in ('W', 'a_src', 'a_dst', 'bias')}
    del _L3_gnn_all
    return {'x': x, 'src': src, 'dst': dst, 'edge_type_32': edge_type_32, 'edge_weight': edge_weight, 'L0_gnn_W_lin': _L0_gnn_in['W_lin'], 'L0_gnn_b_lin': _L0_gnn_in['b_lin'], 'L0_gnn_W_att': _L0_gnn_in['W_att'], 'L0_gnn_b_att': _L0_gnn_in['b_att'], 'L1_gnn_W1': _L1_gnn_in['W1'], 'L1_gnn_b1': _L1_gnn_in['b1'], 'L1_gnn_W2': _L1_gnn_in['W2'], 'L1_gnn_b2': _L1_gnn_in['b2'], 'L2_gnn_W_r': _L2_gnn_in['W_r'], 'L2_gnn_Wq_w': _L2_gnn_in['Wq_w'], 'L2_gnn_Wq_b': _L2_gnn_in['Wq_b'], 'L2_gnn_Wk_w': _L2_gnn_in['Wk_w'], 'L2_gnn_Wk_b': _L2_gnn_in['Wk_b'], 'L2_gnn_rule_emb': _L2_gnn_in['rule_emb'], 'L2_gnn_bias': _L2_gnn_in['bias'], 'L2_gnn_ln_gamma': _L2_gnn_in['ln_gamma'], 'L2_gnn_ln_beta': _L2_gnn_in['ln_beta'], 'L2_gnn_rule_ids': _L2_gnn_in['rule_ids'], 'L3_gnn_W': _L3_gnn_in['W'], 'L3_gnn_a_src': _L3_gnn_in['a_src'], 'L3_gnn_a_dst': _L3_gnn_in['a_dst'], 'L3_gnn_bias': _L3_gnn_in['bias']}

def reference(x, src, dst, edge_type_32, edge_weight, L0_gnn_W_lin, L0_gnn_b_lin, L0_gnn_W_att, L0_gnn_b_att, L1_gnn_W1, L1_gnn_b1, L1_gnn_W2, L1_gnn_b2, L2_gnn_W_r, L2_gnn_Wq_w, L2_gnn_Wq_b, L2_gnn_Wk_w, L2_gnn_Wk_b, L2_gnn_rule_emb, L2_gnn_bias, L2_gnn_ln_gamma, L2_gnn_ln_beta, L2_gnn_rule_ids, L3_gnn_W, L3_gnn_a_src, L3_gnn_a_dst, L3_gnn_bias):
    import jax
    import jax.numpy as jnp

    def _L0_gnn_ref(x, edge_index, W_lin, b_lin, W_att, b_att):
        import jax, jax.numpy as jnp
        import numpy as np
        N = 5000
        E = 80000
        IN = 128
        H = 4
        C = 32
        n = x.shape[0]
        row, col = (edge_index[0], edge_index[1])
        xl = x @ W_lin + b_lin
        hc = xl.shape[1]
        s_i = xl @ W_att[:hc]
        s_j = xl @ W_att[hc:]
        alpha = s_i[row] + s_j[col] + b_att
        alpha = jnp.where(alpha >= 0, alpha, 0.2 * alpha)
        amax = jax.ops.segment_max(alpha, row, num_segments=n)
        alpha = jnp.exp(alpha - amax[row])
        asum = jax.ops.segment_sum(alpha, row, num_segments=n)
        alpha = alpha / (asum[row] + 1e-16)
        xh = xl.reshape(n, H, C)
        msg = alpha[:, :, None] * xh[row]
        out = jax.ops.segment_sum(msg, col, num_segments=n)
        deg = jax.ops.segment_sum(jnp.ones((row.shape[0],), xl.dtype), col, num_segments=n)
        out = jnp.where(deg[:, None, None] > 0, out, xh)
        return out.reshape(n, H * C)

    def _L1_gnn_ref(x, edge_index, edge_weight, W1, b1, W2, b2):
        import jax, jax.numpy as jnp
        import numpy as np
        EPS = 0.0
        N = x.shape[0]
        src, dst = (edge_index[0], edge_index[1])
        msg = edge_weight[:, None] * x[src]
        agg = jax.ops.segment_sum(msg, dst, num_segments=N)
        out = (1.0 + EPS) * x + agg
        h = jax.nn.relu(out @ W1 + b1)
        return h @ W2 + b2

    def _L2_gnn_ref(x, W_r, Wq_w, Wq_b, Wk_w, Wk_b, rule_emb, bias, ln_gamma, ln_beta, src, dst, edge_type, rule_ids):
        import jax, jax.numpy as jnp
        import numpy as np
        N = 3750
        E = 120000
        DIN = 128
        DOUT = 128
        R = 32
        NUM_RULES = 100
        ACTIVE = 4
        EPS = 1e-05
        n_nodes, _ = x.shape
        n_rel, _, dout = W_r.shape
        scale = 1.0 / jnp.sqrt(jnp.float32(dout))
        h_R = rule_emb[rule_ids]
        q = (x @ Wq_w + Wq_b)[dst]
        Wk1, Wk2, Wk3 = jnp.split(Wk_w, 3, axis=0)
        h_rel = W_r.mean(axis=-1)
        k_node = x @ Wk1
        k_rel = h_rel @ Wk2
        v_rule = h_R @ Wk3
        k_base = k_node[src] + k_rel[edge_type] + Wk_b
        score_base = jnp.sum(q * k_base, axis=-1)
        scores = (score_base[:, None] + q @ v_rule.T) * scale
        seg = edge_type * n_nodes + dst
        nseg = n_rel * n_nodes
        m = jax.ops.segment_max(scores, seg, num_segments=nseg)
        ex = jnp.exp(scores - m[seg])
        s = jax.ops.segment_sum(ex, seg, num_segments=nseg)
        attn = ex / s[seg]
        attn_mean = attn.mean(axis=-1)
        proj = jnp.einsum('nd,rdo->nro', x, W_r)
        msg = proj[src, edge_type] * attn_mean[:, None]
        out = jax.ops.segment_sum(msg, dst, num_segments=n_nodes) + bias
        mu = out.mean(axis=-1, keepdims=True)
        var = out.var(axis=-1, keepdims=True)
        out = (out - mu) * jax.lax.rsqrt(var + EPS) * ln_gamma + ln_beta
        return jax.nn.relu(out)

    def _L3_gnn_ref(x, edge_index, W, a_src, a_dst, bias):
        import jax, jax.numpy as jnp
        import numpy as np
        N = 12500
        E = 200000
        D_IN = 128
        D_OUT = 128
        NEG_SLOPE = 0.2
        ALPHA = 0.2
        n = x.shape[0]
        loops = jnp.arange(n, dtype=edge_index.dtype)
        src = jnp.concatenate([edge_index[0], loops])
        dst = jnp.concatenate([edge_index[1], loops])
        h = x @ W
        s_src = h @ a_src
        s_dst = h @ a_dst
        e = jax.nn.leaky_relu(s_src[src] + s_dst[dst], NEG_SLOPE)
        m = jax.ops.segment_max(e, dst, num_segments=n)
        ex = jnp.exp(e - m[dst])
        denom = jax.ops.segment_sum(ex, dst, num_segments=n)
        alpha = ex / denom[dst]
        out = jax.ops.segment_sum(h[src] * alpha[:, None], dst, num_segments=n) + bias
        return jax.nn.leaky_relu(out, ALPHA)
    edge_index = jnp.stack([src, dst])
    x = _layernorm(x + _L0_gnn_ref(x, edge_index, L0_gnn_W_lin, L0_gnn_b_lin, L0_gnn_W_att, L0_gnn_b_att), axis=-1)
    x = _layernorm(x + _L1_gnn_ref(x, edge_index, edge_weight, L1_gnn_W1, L1_gnn_b1, L1_gnn_W2, L1_gnn_b2), axis=-1)
    x = _layernorm(x + _L2_gnn_ref(x, L2_gnn_W_r, L2_gnn_Wq_w, L2_gnn_Wq_b, L2_gnn_Wk_w, L2_gnn_Wk_b, L2_gnn_rule_emb, L2_gnn_bias, L2_gnn_ln_gamma, L2_gnn_ln_beta, src, dst, edge_type_32, L2_gnn_rule_ids), axis=-1)
    x = _layernorm(x + _L3_gnn_ref(x, edge_index, L3_gnn_W, L3_gnn_a_src, L3_gnn_a_dst, L3_gnn_bias), axis=-1)
    return x

_drawn_inputs = setup_inputs


def setup_inputs(seed=0):
    import zlib

    import numpy as np

    out = dict(_drawn_inputs(seed))
    spreads = {'L0_gnn_b_lin': (0.0, 0.1),
     'L0_gnn_b_att': (0.0, 0.8),
     'L1_gnn_b1': (0.0, 0.1),
     'L1_gnn_b2': (0.0, 0.1),
     'L2_gnn_Wq_b': (0.0, 0.8),
     'L2_gnn_Wk_b': (0.0, 0.8),
     'L2_gnn_bias': (0.0, 0.1),
     'L2_gnn_ln_gamma': (1.0, 0.2),
     'L2_gnn_ln_beta': (0.0, 0.1),
     'L3_gnn_bias': (0.0, 0.1)}
    factors = {'L2_gnn_rule_emb': 8.0}
    for name, (base, spread) in spreads.items():
        noise = np.random.default_rng([zlib.crc32(name.encode()), seed]).standard_normal(out[name].shape)
        drawn = base * np.exp(spread * noise) if base else spread * noise
        out[name] = jnp.asarray(drawn.astype(out[name].dtype))
    for name, factor in factors.items():
        out[name] = (out[name] * factor).astype(out[name].dtype)
    return out
```

```python
from contextlib import ExitStack

import concourse.bass as bass
from concourse import mybir

P = 128
D = 128
N_NODES = 6250
N_EDGES = 100000
HEADS = 4
TYPES = 32
RULES = 4
NB = 50
NP = P * NB
NREAL = N_NODES // NB
NC = 784
EP = P * NC
EFULL = N_EDGES // NC
EREST = N_EDGES - EFULL * NC
U = 8
STEPS = NC // (2 * U)
PAD_NODE = NP - 1
MAGIC = 12582912.0
BIG = 1.0e38
ROW0 = 144
QROW = D + TYPES + RULES

ALU = mybir.AluOpType
ACT = mybir.ActivationFunctionType
F32 = mybir.dt.float32
BF16 = mybir.dt.bfloat16
I32 = mybir.dt.int32
AX = mybir.AxisListType.X


class Space:

    def __init__(self, nc, name):
        self.nc, self.name, self.ctx, self.sems = nc, name, ExitStack(), []

    def __enter__(self):
        self.ctx.__enter__()
        return self

    def __exit__(self, *a):
        if self.sems and a[0] is None:
            self.nc.clear_and_free_semaphores(self.sems)
            self.nc.all_engine_barrier()
        return self.ctx.__exit__(*a)

    def sb(self, name, shape, dt=F32):
        return self.ctx.enter_context(self.nc.sbuf_tensor(f"{self.name}_{name}", shape, dt))

    def ps(self, name, shape, dt=F32):
        return self.ctx.enter_context(self.nc.psum_tensor(f"{self.name}_{name}", shape, dt))

    def sem(self, name):
        self.sems.append(self.nc.alloc_semaphore(f"{self.name}_{name}"))
        return self.sems[-1]

    def block(self):
        return self.nc.Block()


def hold(eng, sem, value):
    eng.wait_ge(sem, value)
    eng.nop(nofuse=True)


class Chain:

    def __init__(self, eng, sem):
        self.eng, self.sem, self.n, self.step, self.per, self.k = eng, sem, 0, None, 0, 0

    def loop(self, step, per):
        self.step, self.per, self.k = step, per, 0

    def end(self, count):
        assert self.k == self.per, (self.k, self.per)
        self.n += count * self.per
        self.step = None

    def add(self, ins):
        ins.then_inc(self.sem, 1)
        if self.step is None:
            self.n += 1
        else:
            self.k += 1

    def value(self, back=0):
        return self.n - back if self.step is None else self.step * self.per + (self.n + self.k - back)

    def until(self, back=0, alone=False):
        self.eng.wait_ge(self.sem, self.value(back))
        if alone:
            self.eng.nop(nofuse=True)

    def __call__(self, ins, alone=False):
        self.add(ins)
        self.until(0, alone)


def bc_mid(ap, n):
    return ap.unsqueeze(1).to_broadcast([ap.shape[0], n, ap.shape[1]])


def bc_last(ap, n):
    return ap.unsqueeze(2).to_broadcast([ap.shape[0], ap.shape[1], n])


def bc_last3(ap, n):
    return ap.unsqueeze(3).to_broadcast([ap.shape[0], ap.shape[1], ap.shape[2], n])


def col(ap2, lo, n):
    return ap2[:, bass.ds(lo, n)]


def rounded(dve, chain, out, src, scale, shift):
    chain(dve.tensor_scalar(out, src, scale, shift, ALU.mult, ALU.add))
    chain(dve.tensor_scalar(out, out, MAGIC, None, ALU.add))
    chain(dve.tensor_scalar(out, out, MAGIC, None, ALU.subtract))



def load_inputs(nc, g, x, src, dst, etype, weight):
    with Space(nc, "load") as s:
        raw = s.sb("raw", [P, 4, NC], I32)
        ipart = s.sb("ipart", [P, 1], I32)
        irow = s.sb("irow", [P, P], I32)
        zero = g.zero
        loaded, ready, io, filled = s.sem("loaded"), s.sem("ready"), s.sem("io"), s.sem("filled")
        vs = s.sem("vs")
        zs = [(g.spread_s, 4), (g.spread_0, 4), (g.spread_3, 4)]
        with s.block() as block:
            @block.gpsimd
            def _(pool):
                nc.gpsimd.iota(ipart[:], pattern=[[0, 1]], base=0, channel_multiplier=1).then_inc(io, 1)
                nc.gpsimd.iota(irow[:], pattern=[[1, P]], base=0, channel_multiplier=0).then_inc(io, 1)

            @block.vector
            def _(eng):
                v = nc.vector
                chain = Chain(eng, vs)
                chain(v.memset(zero[:], 0.0))
                chain(v.memset(g.x[:], 0.0))
                chain(v.memset(raw[:, 0:2, :], PAD_NODE))
                chain(v.memset(raw[:, 2:4, :], 0))
                v.memset(g.zmat[:], 0.0)
                v.memset(g.ones[:], 1.0).then_inc(ready, 1)
                eng.wait_ge(io, 2)
                v.tensor_copy(g.part[:], ipart[:]).then_inc(vs, 1)
                chain.n += 1
                chain(v.tensor_copy(g.iota[:], irow[:]))
                v.tensor_scalar(g.ident[:], g.iota[:], g.part[:, 0:1], None, ALU.is_equal)
                v.tensor_scalar(g.identb[:], g.iota[:], g.part[:, 0:1], None, ALU.is_equal)
                v.tensor_scalar(g.after[:], g.iota[:], g.part[:, 0:1], None, ALU.is_gt)
                eng.wait_ge(loaded, 16 * 9)
                for k in range(3):
                    v.tensor_copy(g.rec[:, :, k], raw[:, k, :])
                v.tensor_copy(g.rec[:, :, 3], raw[:, 3, :].bitcast(F32))

            @block.sync
            def _(sp):
                sp.wait_ge(ready, 1)
                sp.dma_start(g.x[0:NREAL, :, :], x.rearrange("(p b) f -> p b f", b=NB)).then_inc(loaded, 16)
                for k, a in enumerate((src, dst, etype, weight)):
                    w = (lambda ap: ap.bitcast(F32)) if k == 3 else (lambda ap: ap)
                    sp.dma_start(w(raw[0:EFULL, k, :]), a[0:EFULL * NC].rearrange("(p j) -> p j", j=NC)).then_inc(loaded, 16)
                    sp.dma_start(w(raw[EFULL:EFULL + 1, k, 0:EREST]),
                                 a[EFULL * NC:N_EDGES].rearrange("(p j) -> p j", p=1)).then_inc(loaded, 16)
                for buf, w in zs:
                    v = buf[0:EP, :].rearrange("(p j) w -> p (j w)", j=NC)
                    for lo in range(0, NC * w, U * QROW):
                        n = min(U * QROW, NC * w - lo)
                        sp.dma_start(v[:, lo:lo + n], zero[:, 0:n]).then_inc(filled, 16)
                fills = 3 * (-(-NC * 4 // (U * QROW)))
                sp.wait_ge(filled, 16 * fills)
                sp.wait_ge(loaded, 16 * 9)



def digits(nc, s, chain, key, hi, lo):
    v = nc.vector
    rounded(v, chain, hi, key, 1.0 / NB, -(NB - 1) / 2.0 / NB)
    chain(v.scalar_tensor_tensor(lo, hi, -float(NB), key, ALU.mult, ALU.add))


def count_keys(nc, s, g, hi, lo, count, highs, lows):
    with Space(nc, s.name + "cnt") as t:
        oh = t.sb("oh", [P, 2, U, highs], BF16)
        ol = t.sb("ol", [P, 2, U, lows], BF16)
        table = t.ps("table", [P, NB])
        made, used, done = t.sem("made"), t.sem("used"), t.sem("done")
        with t.block() as block:
            @block.vector
            def _(eng):
                v = nc.vector
                with eng.Fori(0, STEPS) as i:
                    for h in range(2):
                        hold(eng, used, 2 * i + h + 1)
                        v.tensor_tensor(oh[:, h], bc_mid(g.iota[:, 0:highs], U), bc_last(col(hi, i * 16 + 8 * h, U), highs), ALU.is_equal)
                        v.tensor_tensor(ol[:, h], bc_mid(g.iota[:, 0:lows], U), bc_last(col(lo, i * 16 + 8 * h, U), lows),
                                        ALU.is_equal).then_inc(made, 1)
                eng.wait_ge(done, 1)
                v.tensor_copy(count, table[:])

            @block.tensor
            def _(pe):
                pe.sem_inc(used, 2)
                nc.tensor.matmul(table[:], g.zmat[:], g.zmat[:, 0:NB], start=True, stop=False)
                with pe.Fori(0, STEPS) as i:
                    for h in range(2):
                        hold(pe, made, 2 * i + h + 1)
                        for u in range(U):
                            mm = nc.tensor.matmul(table[0:highs, 0:lows], oh[:, h, u], ol[:, h, u], start=False, stop=False)
                        mm.then_inc(used, 1)
                nc.tensor.matmul(table[:], g.zmat[:], g.zmat[:, 0:NB], start=False, stop=True).then_inc(done, 1)


def scatter_sorted(nc, s, g, hi, lo, start, payload, width, target, column_major, clear=None, ahead=None):
    with Space(nc, s.name + "sct") as t:
        oh = t.sb("oh", [P, 2, U, P], BF16)
        ol = t.sb("ol", [P, 2, U, NB], BF16)
        oht = t.sb("oht", [P, 2, U, P])
        ohtb = t.sb("ohtb", [P, U, P], BF16)
        same = t.sb("same", [P, 2, U, P], BF16)
        run = t.sb("run", [P, 2, NB])
        sel = t.sb("sel", [P, 2, U, NB])
        pos = t.sb("pos", [P, 2, U])
        tmp = t.sb("tmp", [P, U])
        posi = t.sb("posi", [P, 2, U], I32)
        pay = t.sb("pay", [P, 2, U, width])
        table = t.ps("table", [P, NB])
        tr = [t.ps(f"tr{q}", [P, 4, P], BF16) for q in range(2)]
        gram = [t.ps(f"gram{q}", [P, 4, P]) for q in range(2)]
        look = [t.ps(f"look{q}", [P, U, NB]) for q in range(2)]
        vs = t.sem("vs")
        made, tr_ready, oht_ready, ohtb_ready, gram_ready, same_ready = (t.sem(n) for n in ("made", "trr", "ohtr", "ohtbr", "gramr", "samer"))
        table_ready, run_ready, pos_ready, selected, looked = (t.sem(n) for n in ("tabr", "runr", "posr", "seld", "looked"))
        sent = [t.sem(f"sent{h}") for h in range(2)]
        free = [t.sem(f"free{h}") for h in range(2)]
        cleared, offered, tallied, counted = (t.sem(n) for n in ("cleared", "offered", "tallied", "counted"))
        if ahead is not None:
            ahead_hi, ahead_lo, ahead_count = ahead
            oh2, ol2 = t.sb("oh2", [P, 2, U, P], BF16), t.sb("ol2", [P, 2, U, NB], BF16)
            tally = t.ps("tally", [P, NB])
        with t.block() as block:
            @block.vector
            def _(eng):
                v = nc.vector
                chain = Chain(eng, vs)

                def one_hots(h, lo_col):
                    v.tensor_tensor(oh[:, h], bc_mid(g.iota[:], U), bc_last(col(hi, lo_col, U), P), ALU.is_equal)
                    v.tensor_tensor(ol[:, h], bc_mid(g.iota[:, 0:NB], U), bc_last(col(lo, lo_col, U), NB),
                                    ALU.is_equal).then_inc(made, 1)

                def masks(h, wait_gram):
                    for q in range(2):
                        wait_gram(q)
                        v.tensor_tensor(same[:, h, 4 * q:4 * q + 4], gram[q][:], bc_mid(g.after[:], 4), ALU.mult).then_inc(same_ready, 1)

                def select(i, h):
                    hold(eng, looked, 2 * i + (h + 1))
                    v.tensor_tensor(sel[:, h], look[h][:], ol[:, h], ALU.mult).then_inc(selected, 1)
                    hold(eng, selected, 2 * i + h + 1)

                def offer(h, lo_col):
                    v.tensor_tensor(oh2[:, h], bc_mid(g.iota[:], U), bc_last(col(ahead_hi, lo_col, U), P), ALU.is_equal)
                    v.tensor_tensor(ol2[:, h], bc_mid(g.iota[:, 0:NB], U), bc_last(col(ahead_lo, lo_col, U), NB),
                                    ALU.is_equal).then_inc(offered, 1)

                one_hots(0, 0)
                one_hots(1, U)
                if ahead is not None:
                    offer(0, 0)
                    offer(1, U)
                masks(0, lambda q: eng.wait_ge(gram_ready, q + 1))
                with eng.Fori(0, STEPS) as i:
                    chain.loop(i, 2 * (2 + (5 if column_major else 0)))
                    for h in range(2):
                        masks(1 - h, lambda q: hold(eng, gram_ready, 4 * i + (2 * h + q + 3)))
                        select(i, h)
                        one_hots(h, i * 16 + (8 * h + 16))
                        chain(v.tensor_reduce(pos[:, h], sel[:, h], AX, ALU.add))
                        if column_major:
                            chain(v.tensor_scalar(tmp[:], pos[:, h], 1.0 / P, -(P - 1) / 2.0 / P, ALU.mult, ALU.add))
                            chain(v.tensor_scalar(tmp[:], tmp[:], MAGIC, None, ALU.add))
                            chain(v.tensor_scalar(tmp[:], tmp[:], MAGIC, None, ALU.subtract))
                            chain(v.scalar_tensor_tensor(pos[:, h], tmp[:], -float(P), pos[:, h], ALU.mult, ALU.add))
                            chain(v.scalar_tensor_tensor(pos[:, h], pos[:, h], float(NC), tmp[:], ALU.mult, ALU.add))
                        hold(eng, free[h], i + 1)
                        chain(v.tensor_copy(posi[:, h], pos[:, h]))
                        v.tensor_copy(pay[:, h], payload[:, bass.ds(i * 16 + 8 * h, U), :]).then_inc(pos_ready, 1)
                        if ahead is not None:
                            hold(eng, tallied, 2 * i + h + 1)
                            offer(h, i * 16 + (8 * h + 16))
                if ahead is not None:
                    eng.wait_ge(counted, 1)
                    v.tensor_copy(ahead_count, tally[:])

            @block.tensor
            def _(pe):
                def transposes(h):
                    for q in range(2):
                        for u in range(4):
                            mm = nc.tensor.transpose(tr[q][:, u], oh[:, h, 4 * q + u], g.identb[:])
                        mm.then_inc(tr_ready, 1)

                def grams(h, wait_oht):
                    for q in range(2):
                        wait_oht(q)
                        for u in range(4):
                            k = 4 * q + u
                            mm = nc.tensor.matmul(gram[q][:, u], ohtb[:, k], ohtb[:, k], start=True, stop=True)
                        mm.then_inc(gram_ready, 1)

                def look_ups(i, h, q):
                    for u in range(4 * q, 4 * q + 4):
                        hold(pe, run_ready, 16 * i + (8 * h + u + 1))
                        nc.tensor.matmul(table[:], oh[:, h, u], ol[:, h, u], start=False, stop=True,
                                         skip_group_check=True).then_inc(table_ready, 1)
                        if u % 4 == 0:
                            hold(pe, oht_ready, 4 * i + (2 * h + q + 1))
                            hold(pe, same_ready, 4 * i + (2 * h + q + 1))
                        nc.tensor.matmul(look[h][:, u], oht[:, h, u], run[:, u % 2], start=True, stop=False)
                        mm = nc.tensor.matmul(look[h][:, u], same[:, h, u], ol[:, h, u], start=False, stop=True)
                    if q == 1:
                        mm.then_inc(looked, 1)

                if ahead is not None:
                    nc.tensor.matmul(tally[:], g.zmat[:], g.zmat[:, 0:NB], start=True, stop=False)
                nc.tensor.matmul(table[:], g.ident[:], start, start=True, stop=True).then_inc(table_ready, 1)
                pe.wait_ge(made, 1)
                transposes(0)
                grams(0, lambda q: pe.wait_ge(ohtb_ready, q + 1))
                with pe.Fori(0, STEPS) as i:
                    for h in range(2):
                        look_ups(i, h, 0)
                        hold(pe, made, 2 * i + (h + 2))
                        transposes(1 - h)
                        if ahead is not None:
                            hold(pe, offered, 2 * i + (h + 1))
                            for u in range(U):
                                mm = nc.tensor.matmul(tally[:], oh2[:, h, u], ol2[:, h, u], start=False, stop=False)
                            mm.then_inc(tallied, 1)
                        look_ups(i, h, 1)
                        grams(1 - h, lambda q: hold(pe, ohtb_ready, 4 * i + (2 * h + q + 3)))
                if ahead is not None:
                    nc.tensor.matmul(tally[:], g.zmat[:], g.zmat[:, 0:NB], start=False, stop=True).then_inc(counted, 1)

            @block.scalar
            def _(act):
                def transposed(wait_tr):
                    for q in range(2):
                        wait_tr(q)
                        nc.scalar.copy(ohtb[:, 4 * q:4 * q + 4], tr[q][:]).then_inc(ohtb_ready, 1)

                def widened(h):
                    for q in range(2):
                        nc.scalar.copy(oht[:, h, 4 * q:4 * q + 4], tr[q][:]).then_inc(oht_ready, 1)

                def tables(i, h, q):
                    for u in range(4 * q, 4 * q + 4):
                        hold(act, table_ready, 16 * i + (8 * h + u + 1))
                        nc.scalar.copy(run[:, u % 2], table[:]).then_inc(run_ready, 1)

                transposed(lambda q: act.wait_ge(tr_ready, q + 1))
                widened(0)
                with act.Fori(0, STEPS) as i:
                    for h in range(2):
                        tables(i, h, 0)
                        transposed(lambda q: hold(act, tr_ready, 4 * i + (2 * h + q + 3)))
                        tables(i, h, 1)
                        widened(1 - h)

            @block.gpsimd
            def _(pool):
                with pool.Fori(0, STEPS) as i:
                    for h in range(2):
                        hold(pool, pos_ready, 2 * i + h + 1)
                        for u in range(U):
                            nc.gpsimd.indirect_dma_start(
                                out=target, out_offset=bass.IndirectOffsetOnAxis(ap=posi[:, h, u:u + 1], axis=0),
                                in_=pay[:, h, u, :], in_offset=None).then_inc(sent[h], 16)
                for h in range(2):
                    pool.wait_ge(sent[h], 16 * U * STEPS)

            @block.sync
            def _(sp):
                for h in range(2):
                    sp.sem_inc(free[h], 1)
                with sp.Fori(0, STEPS) as i:
                    for h in range(2):
                        if clear is not None:
                            sp.dma_start(clear[0:EP, :].rearrange("(p j) w -> p (j w)", j=NC)[:, bass.ds(i * (2 * U * QROW) + h * U * QROW, U * QROW)],
                                         g.zero[:]).then_inc(cleared, 16)
                        hold(sp, sent[h], i * (16 * U) + 16 * U)
                        sp.sem_inc(free[h], 1)
                if clear is not None:
                    sp.wait_ge(cleared, 16 * 2 * STEPS)


def reload_rows(nc, name, dst, table, width):
    with Space(nc, name) as s:
        got = s.sem("got")
        with s.block() as block:
            @block.sync
            def _(sp):
                sp.dma_start(dst, table[0:EP, :].rearrange("(p j) w -> p j w", j=NC)).then_inc(got, 16)
                sp.wait_ge(got, 16)


def split_keys(nc, name, key, hi, lo):
    with Space(nc, name) as s:
        vs = s.sem("vs")
        with s.block() as block:
            @block.vector
            def _(eng):
                chain = Chain(eng, vs)
                chain(nc.vector.memset(hi[:], 0.0))
                chain(nc.vector.memset(lo[:], 0.0))
                digits(nc, s, chain, key, hi[:, 0:NC], lo[:, 0:NC])


def first_positions(nc, name, g, count, start):
    with Space(nc, name) as s:
        off, upto = s.ps("off", [P, 1]), s.sb("upto", [P, NB])
        vs, tot, offd = s.sem("vs"), s.sem("tot"), s.sem("offd")
        with s.block() as block:
            @block.vector
            def _(eng):
                v = nc.vector
                chain = Chain(eng, vs)
                v.tensor_tensor_scan(upto[:], g.ones[:, 0:NB], count, 0.0, ALU.mult, ALU.add).then_inc(tot, 1)
                eng.wait_ge(tot, 1)
                eng.wait_ge(offd, 1)
                chain(v.tensor_tensor(upto[:], upto[:], count, ALU.subtract))
                chain(v.tensor_scalar(start, upto[:], off[:, 0:1], None, ALU.add))

            @block.tensor
            def _(pe):
                pe.wait_ge(tot, 1)
                nc.tensor.matmul(off[:], g.after[:], upto[:, NB - 1:NB], start=True, stop=True).then_inc(offd, 1)


def sort_by(nc, name, g, key, payload, width, target, column_major, count, start, types=False, clear=None, ahead=None):
    with Space(nc, name) as s:
        hi = s.sb("hi", [P, NC + 2 * U])
        lo = s.sb("lo", [P, NC + 2 * U])
        split_keys(nc, name + "k", key, hi, lo)
        if types:
            count_keys(nc, s, g, hi, lo, count, TYPES, 1)
        first_positions(nc, name + "f", g, count, start)
        if ahead is None:
            scatter_sorted(nc, s, g, hi, lo, start, payload, width, target, column_major, clear)
        else:
            hi2, lo2 = s.sb("hi2", [P, NC + 2 * U]), s.sb("lo2", [P, NC + 2 * U])
            split_keys(nc, name + "a", ahead[0], hi2, lo2)
            scatter_sorted(nc, s, g, hi, lo, start, payload, width, target, column_major, clear, (hi2, lo2, ahead[1]))



def mark_segments(nc, name, g, key, keep, keep_back, full, full_back, keep_max=None, keep_back_max=None):
    with Space(nc, name) as s:
        edge = s.sb("edge", [P, 4])
        rows = s.ps("rows", [1, 4, P])
        bc = s.ps("bc", [P, 2, P])
        row = s.sb("row", [1, 4, P])
        nbr = s.ps("nbr", [P, 2])
        mm1, mm2, mm3, vs, a1, a2 = (s.sem(n) for n in ("m1", "m2", "m3", "vs", "a1", "a2"))
        with s.block() as block:
            @block.vector
            def _(eng):
                v = nc.vector
                chain = Chain(eng, vs)
                v.tensor_copy(edge[:, 0:1], key[:, 0:1])
                v.tensor_copy(edge[:, 1:2], key[:, NC - 1:NC]).then_inc(a1, 1)
                v.tensor_tensor(keep[:, 1:NC], key[:, 1:NC], key[:, 0:NC - 1], ALU.is_equal)
                chain(v.tensor_tensor(keep_back[:, 0:NC - 1], key[:, 1:NC], key[:, 0:NC - 1], ALU.is_equal))
                eng.wait_ge(mm1, 1)
                chain(v.memset(row[:], -1.0))
                v.tensor_copy(row[:, 0, 1:P], rows[:, 1, 0:P - 1])
                v.tensor_copy(row[:, 1, 0:P - 1], rows[:, 0, 1:P]).then_inc(a2, 1)
                eng.wait_ge(mm2, 1)
                v.tensor_tensor(keep[:, 0:1], key[:, 0:1], nbr[:, 0:1], ALU.is_equal)
                chain(v.tensor_tensor(keep_back[:, NC - 1:NC], key[:, NC - 1:NC], nbr[:, 1:2], ALU.is_equal))
                chain(v.tensor_reduce(edge[:, 2:3], keep[:], AX, ALU.min))
                v.tensor_reduce(edge[:, 3:4], keep_back[:], AX, ALU.min).then_inc(a2, 1)
                eng.wait_ge(mm3, 1)
                v.tensor_copy(full[:], bc[:, 0, :])
                v.tensor_copy(full_back[:], bc[:, 1, :])

            @block.tensor
            def _(pe):
                pe.wait_ge(a1, 1)
                for k in range(2):
                    mm = nc.tensor.matmul(rows[:, k, :], edge[:, k:k + 1], g.ident[:], start=True, stop=True)
                mm.then_inc(mm1, 1)
                pe.wait_ge(a2, 1)
                for k in range(2):
                    mm = nc.tensor.matmul(nbr[:, k:k + 1], row[0:1, k, :], g.ones[0:1, 0:1], start=True, stop=True)
                mm.then_inc(mm2, 1)
                pe.wait_ge(a2, 2)
                for k in range(2):
                    mm = nc.tensor.matmul(bc[:, k, :], edge[:, 2 + k:3 + k].to_broadcast([P, P]), g.ident[:], start=True, stop=True)
                mm.then_inc(mm3, 1)


def segment_scan(nc, name, g, vals, outs, keep, full, op, reverse=False):
    W = len(vals)
    maximum = op == ALU.max
    op0 = ALU.add if maximum else ALU.mult
    with Space(nc, name) as s:
        last = s.sb("last", [P, W])
        lastT = s.ps("lastT", [W, P])
        fullx = s.sb("fullx", [W, P])
        carry = s.sb("carry", [W, P])
        shifted = s.sb("shifted", [W, P])
        back = s.ps("back", [P, W])
        init = s.sb("init", [P, W])
        factor, draft = s.sb("factor", [P, NC]), s.sb("draft", [P, NC])
        vs, a1, m1, a2, m2 = (s.sem(n) for n in ("vs", "a1", "m1", "a2", "m2"))
        low = -BIG if maximum else 0.0
        turn = (lambda ap: ap[:, ::-1]) if reverse else (lambda ap: ap)
        edge = 0 if reverse else NC - 1
        with s.block() as block:
            @block.vector
            def _(eng):
                v = nc.vector
                chain = Chain(eng, vs)
                if maximum:
                    v.tensor_scalar(fullx[:], full[0:W, :], BIG, -BIG, ALU.mult, ALU.add)
                    chain(v.tensor_scalar(factor[:], keep, BIG, -BIG, ALU.mult, ALU.add))
                else:
                    v.tensor_copy(fullx[:], full[0:W, :])
                    chain(v.tensor_copy(factor[:], keep))
                for w in range(W):
                    chain(v.tensor_tensor_scan(turn(draft[:]), turn(factor[:]), turn(vals[w]), low, op0, op))
                    chain(v.tensor_copy(last[:, w:w + 1], draft[:, edge:edge + 1]))
                v.memset(shifted[:], low).then_inc(a1, 1)
                eng.wait_ge(a1, 1)
                eng.wait_ge(m1, 1)
                chain(v.tensor_tensor_scan(turn(carry[:]), turn(fullx[:]), turn(lastT[:]), low, op0, op))
                if reverse:
                    v.tensor_copy(shifted[:, 0:P - 1], carry[:, 1:P]).then_inc(a2, 1)
                else:
                    v.tensor_copy(shifted[:, 1:P], carry[:, 0:P - 1]).then_inc(a2, 1)
                eng.wait_ge(m2, 1)
                chain(v.tensor_copy(init[:], back[:]))
                for w in range(W):
                    v.tensor_tensor_scan(turn(outs[w]), turn(factor[:]), turn(vals[w]), init[:, w:w + 1], op0, op)

            @block.tensor
            def _(pe):
                pe.wait_ge(a1, 1)
                nc.tensor.transpose(lastT[:], last[:], g.ident[:]).then_inc(m1, 1)
                pe.wait_ge(a2, 1)
                nc.tensor.transpose(back[:], shifted[:], g.ident[0:W, 0:W]).then_inc(m2, 1)


def segment_total(nc, name, g, order, vals, outs, op):
    segment_scan(nc, name + "f", g, vals, outs, order.keep[:], order.full, op)
    with Space(nc, name) as s:
        isend = s.sb("isend", [P, NC])
        vs = s.sem("vs")
        with s.block() as block:
            @block.vector
            def _(eng):
                v = nc.vector
                chain = Chain(eng, vs)
                chain(v.tensor_scalar(isend[:], order.keep_back[:], -1.0, 1.0, ALU.mult, ALU.add))
                for o in outs:
                    v.tensor_tensor(o, o, isend[:], ALU.mult)
    segment_scan(nc, name + "b", g, outs, outs, order.keep_back[:], order.full_back, ALU.add, reverse=True)


def node_ends(nc, name, g, o, count, start, dst_side):
    with Space(nc, name) as s:
        t = s.sb("t", [P, NB])
        last = s.sb("last", [P, NB])
        empty = s.sb("empty", [P, NB])
        pe_, ps_ = s.sb("pe", [P, NB]), s.sb("ps", [P, NB])
        nid = s.sb("nid", [P, NB], I32)
        vs, io, made, wrote, got = (s.sem(n) for n in ("vs", "io", "made", "wrote", "got"))
        with s.block() as block:
            @block.gpsimd
            def _(pool):
                nc.gpsimd.iota(nid[:], pattern=[[1, NB]], base=EP, channel_multiplier=NB).then_inc(io, 1)

            @block.vector
            def _(eng):
                v = nc.vector
                chain = Chain(eng, vs)
                v.tensor_scalar(o.some[:], count, 0.5, None, ALU.is_gt)
                chain(v.tensor_scalar(empty[:], count, 0.5, None, ALU.is_lt))
                chain(v.tensor_tensor(last[:], start, count, ALU.add))
                chain(v.tensor_scalar(last[:], last[:], -1.0, 0.0, ALU.add, ALU.max))
                v.tensor_copy(o.end_i[:], last[:])
                eng.wait_ge(io, 1)
                chain(v.tensor_copy(t[:], nid[:]))
                chain(v.tensor_tensor(t[:], t[:], start, ALU.subtract))
                chain(v.tensor_tensor(t[:], t[:], empty[:], ALU.mult))
                chain(v.tensor_tensor(t[:], t[:], start, ALU.add))
                chain(v.tensor_copy(o.start_i[:], t[:]))
                if dst_side:
                    rounded(v, chain, pe_[:], last[:], 1.0 / NC, -(NC - 1) / 2.0 / NC)
                    rounded(v, chain, ps_[:], start, 1.0 / NC, -(NC - 1) / 2.0 / NC)
                    chain(v.tensor_tensor(o.span[:], pe_[:], ps_[:], ALU.is_gt))
                    chain(v.tensor_tensor(o.span[:], o.span[:], o.some[:], ALU.mult))
                    chain(v.tensor_tensor(pe_[:], pe_[:], o.span[:], ALU.mult))
                    v.tensor_scalar(pe_[:], pe_[:], -1.0, None, ALU.add).then_inc(made, 1)

            if dst_side:
                @block.sync
                def _(sp):
                    sp.wait_ge(made, 1)
                    sp.dma_start(g.carry_row.rearrange("(p b) -> p b", b=NB), pe_[:]).then_inc(wrote, 16)
                    sp.wait_ge(wrote, 16)


class Order:

    def __init__(self, s, name):
        self.keep = s.sb(name + "keep", [P, NC])
        self.keep_back = s.sb(name + "keepb", [P, NC])
        self.full = s.sb(name + "full", [P, P])
        self.full_back = s.sb(name + "fullb", [P, P])
        self.some = s.sb(name + "some", [P, NB])
        self.span = s.sb(name + "span", [P, NB])
        self.end_i = s.sb(name + "endi", [P, NB], I32)
        self.start_i = s.sb(name + "starti", [P, NB], I32)


def gather_at_nodes(nc, name, table, idx, out, width):
    with Space(nc, name) as s:
        got = s.sem("got")
        with s.block() as block:
            @block.gpsimd
            def _(pool):
                for b in range(NB):
                    nc.gpsimd.indirect_dma_start(out=out[:, b, :], out_offset=None, in_=table,
                                                 in_offset=bass.IndirectOffsetOnAxis(ap=idx[:, b:b + 1], axis=0)).then_inc(got, 16)
                pool.wait_ge(got, 16 * NB)


def spread_scalars(nc, name, g, order, nodes, width, table, first_key, zeros, outs):
    with Space(nc, name) as s:
        wide = s.sb("wide", [P, NC, width])
        first = s.sb("first", [P, 1], I32)
        init = s.sb("init", [P, width])
        stored, sent, got, vi, ls = (s.sem(n) for n in ("stored", "sent", "got", "vi", "ls"))
        with s.block() as block:
            @block.vector
            def _(eng):
                nc.vector.tensor_copy(first[:], first_key).then_inc(vi, 1)
                eng.wait_ge(got, 16)
                eng.wait_ge(ls, 16)
                for w in [k for k, o in enumerate(outs) if o is not None]:
                    nc.vector.tensor_tensor_scan(outs[w], order.keep[:], wide[:, :, w], init[:, w:w + 1], ALU.mult, ALU.add)

            @block.gpsimd
            def _(pool):
                for b in range(NB):
                    nc.gpsimd.indirect_dma_start(out=zeros, out_offset=bass.IndirectOffsetOnAxis(ap=order.start_i[:, b:b + 1], axis=0),
                                                 in_=nodes[:, b, :], in_offset=None).then_inc(sent, 16)
                pool.wait_ge(stored, 16)
                pool.wait_ge(vi, 1)
                nc.gpsimd.indirect_dma_start(out=init[:], out_offset=None, in_=table,
                                             in_offset=bass.IndirectOffsetOnAxis(ap=first[:, 0:1], axis=0)).then_inc(got, 16)
                pool.wait_ge(sent, 16 * NB)

            @block.sync
            def _(sp):
                sp.dma_start(table.rearrange("(p b) w -> p b w", b=NB), nodes).then_inc(stored, 16)
                sp.wait_ge(sent, 16 * NB)
                sp.dma_start(wide[:], zeros[0:EP, :].rearrange("(p j) w -> p j w", j=NC)).then_inc(ls, 16)
                sp.wait_ge(ls, 16)
                sp.wait_ge(stored, 16)



def sum_messages(nc, name, g, order, table, width, index, weigh):
    with Space(nc, name) as s:
        rows = s.sb("rows", [P, 2, U, width])
        msg = s.sb("msg", [P, 2, U, D])
        acc = s.sb("acc", [P, 2, U, D])
        idx = s.sb("idx", [P, 2, U], I32)
        factor = s.sb("factor", [P, 2, U])
        vs, us, es = s.sem("vs"), s.sem("us"), s.sem("es")
        idx_ready = [s.sem(f"idxr{h}") for h in range(2)]
        got = [s.sem(f"got{h}") for h in range(2)]
        acc_ready = [s.sem(f"accr{h}") for h in range(2)]
        stored = [s.sem(f"sto{h}") for h in range(2)]
        acc_free = [s.sem(f"accf{h}") for h in range(2)]
        w = weigh(nc, s, us, es, order, rows, msg, factor)
        half = D // 2
        with s.block() as block:
            @block.vector
            def _(eng):
                v = nc.vector
                chain = Chain(eng, vs)
                for h in range(2):
                    v.tensor_copy(idx[:, h], index[:, U * h:U * h + U]).then_inc(idx_ready[h], 1)
                chain(v.memset(acc[:], 0.0))
                w.start(chain)
                with eng.Fori(0, STEPS) as i:
                    chain.loop(i, 2 * (w.dve_steps + 2 * U - 1))
                    for h in range(2):
                        hold(eng, got[h], i * (16 * U) + 16 * U)
                        w.dve(eng, chain, i, h)
                        hold(eng, acc_free[h], i + 1)
                        for u in range(U):
                            for f in range(2):
                                if u:
                                    chain.until(1)
                                c = slice(f * half, (f + 1) * half)
                                prev = acc[:, h, u - 1, c] if u else acc[:, 1 - h, U - 1, c]
                                ins = v.scalar_tensor_tensor(acc[:, h, u, c], prev, factor[:, h, u:u + 1],
                                                             msg[:, h, u, c], ALU.mult, ALU.add)
                                if u == U - 1 and f == 1:
                                    ins.then_inc(acc_ready[h], 1)
                                else:
                                    chain.add(ins)
                        hold(eng, acc_ready[h], i + 1)
                        v.tensor_copy(idx[:, h], index[:, bass.ds(i * 16 + 16 + 8 * h, U)]).then_inc(idx_ready[h], 1)
                chain.end(STEPS)
                v.tensor_copy(g.tail[:], acc[:, 1, U - 1])

            if w.act:
                @block.scalar
                def _(act):
                    with act.Fori(0, STEPS) as i:
                        for h in range(2):
                            w.act(act, i, h)

            @block.gpsimd
            def _(pool):
                with pool.Fori(0, STEPS) as i:
                    for h in range(2):
                        hold(pool, idx_ready[h], i + 1)
                        for u in range(U):
                            nc.gpsimd.indirect_dma_start(out=rows[:, h, u, :], out_offset=None, in_=table,
                                                         in_offset=bass.IndirectOffsetOnAxis(ap=idx[:, h, u:u + 1], axis=0)).then_inc(got[h], 16)

            @block.sync
            def _(sp):
                out = g.prefix.rearrange("(p j) f -> p (j f)", j=NC)
                for h in range(2):
                    sp.sem_inc(acc_free[h], 1)
                with sp.Fori(0, STEPS) as i:
                    for h in range(2):
                        hold(sp, acc_ready[h], i + 1)
                        sp.dma_start(out[:, bass.ds(i * (2 * U * D) + h * U * D, U * D)],
                                     acc[:, h].rearrange("p u f -> p (u f)")).then_inc(stored[h], 16)
                        hold(sp, stored[h], i * 16 + 16)
                        sp.sem_inc(acc_free[h], 1)


class Weighed:
    dve_steps, act = 1, None

    def __init__(self, weight):
        self.weight = weight

    def __call__(self, nc, s, us, es, order, rows, msg, factor):
        self.rows, self.msg, self.v, self.factor, self.order = rows, msg, nc.vector, factor, order
        return self

    def start(self, chain):
        pass

    def dve(self, eng, chain, i, h):
        c = bass.ds(i * 16 + 8 * h, U)
        self.v.tensor_copy(self.factor[:, h], self.order.keep[:, c])
        chain(self.v.tensor_tensor(self.msg[:, h], self.rows[:, h, :, 0:D], bc_last(self.weight[:, c], D), ALU.mult))


class Attended0:
    dve_steps = 4

    def __init__(self, sj):
        self.sj = sj

    def __call__(self, nc, s, us, es, order, rows, msg, factor):
        self.nc, self.us, self.es = nc, us, es
        self.rows, self.msg, self.v, self.factor, self.order = rows, msg, nc.vector, factor, order
        self.a = s.sb("a", [P, 2, U, HEADS])
        self.b = s.sb("b", [P, 2, U, HEADS])
        return self

    def start(self, chain):
        pass

    def dve(self, eng, chain, i, h):
        v, a, b, rows = self.v, self.a, self.b, self.rows
        c = bass.ds(i * 16 + 8 * h, U)
        sj = self.sj[:, :, c].rearrange("p w j -> p j w")
        v.tensor_copy(self.factor[:, h], self.order.keep[:, c])
        chain(v.tensor_tensor(a[:, h], rows[:, h, :, D:D + 4], sj, ALU.add))
        chain(v.scalar_tensor_tensor(b[:, h], a[:, h], 0.2, a[:, h], ALU.mult, ALU.max))
        v.tensor_tensor(a[:, h], b[:, h], rows[:, h, :, D + 4:D + 8], ALU.subtract).then_inc(self.us, 1)
        hold(eng, self.es, 2 * i + h + 1)
        chain(v.tensor_tensor(a[:, h], b[:, h], rows[:, h, :, D + 8:D + 12], ALU.mult))
        chain(v.tensor_tensor(self.msg[:, h].rearrange("p u (w c) -> p (u w) c", w=HEADS),
                              rows[:, h, :, 0:D].rearrange("p u (w c) -> p u w c", w=HEADS),
                              bc_last3(a[:, h], D // HEADS), ALU.mult))

    def act(self, eng, i, h):
        hold(eng, self.us, 2 * i + h + 1)
        self.nc.scalar.activation(self.b[:, h], self.a[:, h], ACT.Exp).then_inc(self.es, 1)


class Online3:
    dve_steps = 8

    def __init__(self, sd, most, total):
        self.sd, self.most, self.total = sd, most, total

    def __call__(self, nc, s, us, es, order, rows, msg, factor):
        self.nc, self.us, self.es = nc, us, es
        self.rows, self.msg, self.v, self.factor, self.order = rows, msg, nc.vector, factor, order
        self.e = s.sb("e", [P, 2, U])
        self.before = s.sb("before", [P, 2, U])
        self.gap = s.sb("gap", [P, 2, U])
        self.m = s.sb("m", [P, 2, U + 1])
        self.d = s.sb("d", [P, 2, 2, U])
        self.x = s.sb("xx", [P, 2, 2, U])
        self.t = s.sb("t", [P, 2, U])
        return self

    def start(self, chain):
        chain(self.v.memset(self.m[:], -BIG))
        chain(self.v.memset(self.t[:], 0.0))

    def dve(self, eng, chain, i, h):
        v, e, m, gap, d, x, t = self.v, self.e, self.m, self.gap, self.d, self.x, self.t
        c = bass.ds(i * 16 + 8 * h, U)
        v.tensor_scalar(gap[:, h], self.order.keep[:, c], BIG, -BIG, ALU.mult, ALU.add)
        v.tensor_copy(m[:, h, 0:1], m[:, 1 - h, U:U + 1])
        chain(v.tensor_tensor(e[:, h], self.rows[:, h, :, D], self.sd[:, c], ALU.add))
        chain(v.scalar_tensor_tensor(e[:, h], e[:, h], 0.2, e[:, h], ALU.mult, ALU.max))
        chain(v.tensor_tensor_scan(m[:, h, 1:U + 1], gap[:, h], e[:, h], m[:, 1 - h, U:U + 1], ALU.add, ALU.max))
        v.tensor_tensor(d[:, h, 1], e[:, h], m[:, h, 1:U + 1], ALU.subtract)
        chain(v.tensor_tensor(self.before[:, h], gap[:, h], m[:, h, 0:U], ALU.add))
        v.tensor_tensor(d[:, h, 0], self.before[:, h], m[:, h, 1:U + 1], ALU.subtract).then_inc(self.us, 1)
        chain.add(v.tensor_copy(self.most[:, c, 0], m[:, h, 1:U + 1]))
        hold(eng, self.es, 2 * i + h + 1)
        v.tensor_copy(self.factor[:, h], x[:, h, 0])
        chain(v.tensor_tensor(self.msg[:, h], self.rows[:, h, :, 0:D], bc_last(x[:, h, 1], D), ALU.mult))
        chain(v.tensor_tensor_scan(t[:, h], x[:, h, 0], x[:, h, 1], t[:, 1 - h, U - 1:U], ALU.mult, ALU.add), alone=True)
        chain.add(v.tensor_copy(self.total[:, c, 1], t[:, h]))

    def act(self, eng, i, h):
        hold(eng, self.us, 2 * i + h + 1)
        self.nc.scalar.activation(self.x[:, h], self.d[:, h], ACT.Exp).then_inc(self.es, 1)


CHUNK = 10


def finish_sum(nc, name, g, order, agg, online=None):
    with Space(nc, name) as s:
        W = D + 2 if online else D
        tailT = s.ps("tailT", [P, P])
        carry = s.sb("carry", [P, 3, P])
        carryT = s.ps("carryT", [P, 3, P])
        carried = s.sb("carried", [P, W])
        wants = s.sb("wants", [P, NP])
        pick = s.sb("pick", [P, 4, P])
        spread = s.ps("spread", [P, 2, P])
        pre = s.sb("pre", [P, 6, P])
        extra = [s.ps(f"extra{h}", [P, W]) for h in range(4)]
        vs, m1, a1, m2, a2, ld, picked, made, us, es = (s.sem(n) for n in ("vs", "m1", "a1", "m2", "a2", "ld", "picked", "made", "us", "es"))
        got = [s.sem(f"got{k}") for k in range(NB // CHUNK)]
        parts = 3 if online else 1
        with s.block() as block:
            @block.sync
            def _(sp):
                sp.dma_start(wants[:], g.carry_row.rearrange("(o n) -> o n", o=1).broadcast_to([P, NP])).then_inc(ld, 16)
                sp.wait_ge(ld, 16)

            @block.gpsimd
            def _(pool):
                for b in range(NB):
                    nc.gpsimd.indirect_dma_start(out=agg[:, b, :], out_offset=None, in_=g.prefix,
                                                 in_offset=bass.IndirectOffsetOnAxis(ap=order.end_i[:, b:b + 1], axis=0)).then_inc(got[b // CHUNK], 16)

            @block.tensor
            def _(pe):
                if online:
                    for k in range(2):
                        nc.tensor.matmul(spread[:, k], online[k].to_broadcast([P, P]), g.ident[:], start=True, stop=True)
                nc.tensor.transpose(tailT[:], g.tail[:], g.ident[:]).then_inc(m1, 1)
                pe.wait_ge(a1, 1)
                for k in range(parts):
                    mm = nc.tensor.transpose(carryT[:, k], carry[:, k], g.ident[:])
                mm.then_inc(m2, 1)
                pe.wait_ge(a2, 1)
                for b in range(NB):
                    pe.wait_ge(picked, b + 1)
                    nc.tensor.matmul(extra[b % 4][:], pick[:, b % 4], carried[:], start=True, stop=True).then_inc(made, 1)

            if online:
                @block.scalar
                def _(act):
                    act.wait_ge(us, 1)
                    nc.scalar.activation(pre[:, 4:6], pre[:, 2:4], ACT.Exp).then_inc(es, 1)

            @block.vector
            def _(eng):
                v = nc.vector
                chain = Chain(eng, vs)
                eng.wait_ge(m1, 1)
                if online:
                    gap, before, of, op_ = pre[:, 0], pre[:, 1], pre[:, 2], pre[:, 3]
                    v.memset(pre[:, 1], -BIG)
                    v.tensor_scalar(gap, order.full[:], BIG, -BIG, ALU.mult, ALU.add)
                    chain(v.tensor_copy(pre[:, 2], spread[:, 0]))
                    chain(v.tensor_tensor_scan(carry[:, 2], gap, pre[:, 2], -BIG, ALU.add, ALU.max))
                    chain(v.tensor_copy(pre[:, 1, 1:P], carry[:, 2, 0:P - 1]))
                    v.tensor_tensor(of, of, carry[:, 2], ALU.subtract)
                    chain(v.tensor_tensor(before, before, gap, ALU.add))
                    v.tensor_tensor(op_, before, carry[:, 2], ALU.subtract).then_inc(us, 1)
                    eng.wait_ge(es, 1)
                    chain(v.tensor_tensor(gap, tailT[:], pre[:, 4], ALU.mult))
                    v.tensor_tensor_scan(carry[:, 0], pre[:, 5], gap, 0.0, ALU.mult, ALU.add)
                    chain(v.tensor_tensor(before, spread[:, 1], pre[:, 4], ALU.mult))
                    v.tensor_tensor_scan(carry[:, 1], pre[:, 5], before, 0.0, ALU.mult, ALU.add).then_inc(a1, 1)
                else:
                    v.tensor_tensor_scan(carry[:, 0], order.full[:], tailT[:], 0.0, ALU.mult, ALU.add).then_inc(a1, 1)
                eng.wait_ge(m2, 1)
                if online:
                    v.tensor_copy(carried[:, D:D + 1], carryT[:, 1, 0:1])
                    v.tensor_copy(carried[:, D + 1:D + 2], carryT[:, 2, 0:1])
                v.tensor_copy(carried[:, 0:D], carryT[:, 0]).then_inc(a2, 1)
                eng.wait_ge(ld, 16)
                by_node = wants[:].rearrange("p (m b) -> p m b", b=NB)

                def add(b):
                    eng.wait_ge(made, b + 1)
                    if online:
                        v.tensor_copy(online[2][:, b, :], extra[b % 4][:])
                        return
                    if b % CHUNK == 0:
                        eng.wait_ge(got[b // CHUNK], 16 * CHUNK)
                    v.scalar_tensor_tensor(agg[:, b, :], agg[:, b, :], order.some[:, b:b + 1], extra[b % 4][:], ALU.mult, ALU.add)

                for b in range(NB):
                    if b >= 4:
                        add(b - 4)
                    v.tensor_scalar(pick[:, b % 4], by_node[:, :, b], g.part[:, 0:1], None, ALU.is_equal).then_inc(picked, 1)
                for b in range(NB - 4, NB):
                    add(b)
                if online:
                    for k in range(NB // CHUNK):
                        eng.wait_ge(got[k], 16 * CHUNK)



def layernorm(nc, name, y, sq, eps_tile, gamma=None, beta=None, relu=False):
    with Space(nc, name) as s:
        m, r = s.sb("m", [P, NB]), s.sb("r", [P, NB])
        vs, asked, root = s.sem("vs"), s.sem("asked"), s.sem("root")
        with s.block() as block:
            @block.vector
            def _(eng):
                v = nc.vector
                chain = Chain(eng, vs)
                chain(v.tensor_reduce(m[:], y, AX, ALU.add))
                chain(v.tensor_scalar(m[:], m[:], 1.0 / D, None, ALU.mult))
                chain(v.tensor_tensor(y, y, bc_last(m[:], D), ALU.subtract))
                chain(v.tensor_tensor(sq, y, y, ALU.mult))
                v.tensor_reduce(r[:], sq, AX, ALU.add).then_inc(asked, 1)
                eng.wait_ge(root, 1)
                chain(v.reciprocal(m[:], r[:]))
                chain(v.tensor_tensor(y, y, bc_last(m[:], D), ALU.mult))
                if gamma is not None:
                    chain(v.tensor_tensor(y, y, bc_mid(gamma, NB), ALU.mult))
                    chain(v.tensor_tensor(y, y, bc_mid(beta, NB), ALU.add))
                if relu:
                    chain(v.tensor_scalar(y, y, 0.0, None, ALU.max))

            @block.scalar
            def _(act):
                act.wait_ge(asked, 1)
                nc.scalar.activation(r[:], r[:], ACT.Sqrt, bias=eps_tile, scale=1.0 / D).then_inc(root, 1)


def add_nodes(nc, name, x, y):
    with Space(nc, name) as s:
        with s.block() as block:
            @block.vector
            def _(eng):
                nc.vector.tensor_tensor(x, x, y, ALU.add)


def node_loop(nc, s, source, stages):
    K = len(stages)
    pe_done, dve_done, vs, feed = s.sem("ped"), s.sem("dved"), s.sem("nvs"), s.sem("feed")
    fed = s.fed
    with s.block() as block:
        @block.scalar
        def _(act):
            for h in range(2):
                nc.scalar.copy(fed[:, h], source[:, h, :]).then_inc(feed, 1)
            with act.Fori(0, NB // 2 - 1) as i:
                for h in range(2):
                    hold(act, dve_done, i * (2 * K) + (h + 2))
                    nc.scalar.copy(fed[:, h], xcol(source, i * 2 + (2 + h))).then_inc(feed, 1)

        @block.tensor
        def _(pe):
            with pe.Fori(0, NB // 2) as i:
                for k, (pe_part, _, _) in enumerate(stages):
                    for h in range(2):
                        if k == 0:
                            hold(pe, feed, i * 2 + (h + 1))
                        hold(pe, dve_done, i * (2 * K) + (1 + (2 * (k - 1) + h + 1 if k else 0)))
                        pe_part(i * 2 + h, h).then_inc(pe_done, 1)

        @block.vector
        def _(eng):
            chain = Chain(eng, vs)
            eng.sem_inc(dve_done, 1)
            with eng.Fori(0, NB // 2) as i:
                chain.loop(i, 2 * sum(st[2] for st in stages))
                for k, (_, dve_part, _) in enumerate(stages):
                    for h in range(2):
                        hold(eng, pe_done, i * (2 * K) + (2 * k + h + 1))
                        dve_part(chain, i * 2 + h, h).then_inc(dve_done, 1)


def load_weights(nc, name, pairs):
    with Space(nc, name) as s:
        ld = s.sem("ld")
        with s.block() as block:
            @block.sync
            def _(sp):
                for dst, src in pairs:
                    sp.dma_start(dst, src).then_inc(ld, 16)
                sp.wait_ge(ld, 16 * len(pairs))


def row_bc(a):
    return a.rearrange("(o n) -> o n", o=1).broadcast_to([P, a.shape[0]])


def xcol(t, b):
    return t[:, bass.ds(b, 1), :].rearrange("p o f -> p (o f)")


def project_and_score(nc, name, g, w, bias_bc, att, n_att, out, scores):
    with Space(nc, name) as s:
        tp = [s.ps(f"tp{h}", [P, P]) for h in range(2)]
        pm = [s.ps(f"pm{h}", [P, P]) for h in range(2)]
        tq = [s.ps(f"tq{h}", [P, P]) for h in range(2)]
        sc = [s.ps(f"sc{h}", [P, n_att]) for h in range(2)]
        xT, oT, o = s.sb("xT", [P, 2, P]), s.sb("oT", [P, 2, P]), s.sb("o", [P, 2, P])
        s.fed = s.sb("fed", [P, 2, P])
        t, v = nc.tensor, nc.vector

        def take(chain, b, h):
            if bias_bc is None:
                chain(v.tensor_copy(o[:, h], pm[h][:]))
            else:
                chain(v.tensor_tensor(o[:, h], pm[h][:], bias_bc, ALU.add))
            return v.tensor_copy(xcol(out, b), o[:, h])

        node_loop(nc, s, g.x, [
            (lambda b, h: t.transpose(tp[h][:], s.fed[:, h], g.ident[:]), lambda c, b, h: v.tensor_copy(xT[:, h], tp[h][:]), 0),
            (lambda b, h: t.matmul(pm[h][:], xT[:, h], w, start=True, stop=True), take, 1),
            (lambda b, h: t.transpose(tq[h][:], o[:, h], g.ident[:]), lambda c, b, h: v.tensor_copy(oT[:, h], tq[h][:]), 0),
            (lambda b, h: t.matmul(sc[h][:], oT[:, h], att, start=True, stop=True), lambda c, b, h: v.tensor_copy(xcol(scores, b), sc[h][:]), 0),
        ])


def store_rows(nc, name, pairs):
    load_weights(nc, name, pairs)


def by_nodes(table):
    return table.rearrange("(p b) w -> p b w", b=NB)


def layer0(nc, g, O, a):
    with Space(nc, "l0") as s:
        xl = s.sb("xl", [P, NB, D])
        row = s.sb("row", [P, NB, 16])
        sj_d = s.sb("sjd", [P, HEADS, NC])
        with Space(nc, "l0a") as q:
            w, att, bias, batt = q.sb("w", [P, D]), q.sb("att", [P, 2, HEADS]), q.sb("bias", [P, D]), q.sb("batt", [P, HEADS])
            scores, sjn = q.sb("scores", [P, NB, 2 * HEADS]), q.sb("sjn", [P, NB, HEADS])
            load_weights(nc, "l0w", [(w[:], a["L0_gnn_W_lin"]), (att[:], a["L0_gnn_W_att"].rearrange("(t k) h -> k t h", t=2)),
                                     (bias[:], row_bc(a["L0_gnn_b_lin"])), (batt[:], row_bc(a["L0_gnn_b_att"]))])
            project_and_score(nc, "l0p", g, w[:], bias[:], att[:].rearrange("p t h -> p (t h)"), 2 * HEADS, xl, scores)
            with q.block() as block:
                @block.vector
                def _(eng):
                    nc.vector.tensor_tensor(row[:, :, 0:4], scores[:, :, 0:4], bc_mid(batt[:], NB), ALU.add)
                    nc.vector.tensor_copy(sjn[:], scores[:, :, 4:8])
            spread_scalars(nc, "l0d", g, O.dst, sjn[:], HEADS, g.scores0, g.dst[:, 0:1], g.spread_0, [sj_d[:, k, :] for k in range(HEADS)])
        with Space(nc, "l0b") as q:
            recs = q.sb("recs", [P, NC, 8])
            src_s = q.sb("srcs", [P, NC])
            start = q.sb("start", [P, NB])
            with q.block() as block:
                @block.vector
                def _(eng):
                    nc.vector.tensor_copy(recs[:, :, 0], g.src[:, 0:NC])
                    for k in range(HEADS):
                        nc.vector.tensor_copy(recs[:, :, 1 + k], sj_d[:, k, :])
                    nc.vector.memset(recs[:, :, 5:8], 0.0)
            sort_by(nc, "l0s", g, g.src[:, 0:NC], recs, 8, g.by_src, False, g.count_src[:], start[:])
            reload_rows(nc, "l0r", recs[:], g.by_src, 8)
            order = Order(q, "so")
            with q.block() as block:
                @block.vector
                def _(eng):
                    nc.vector.tensor_copy(src_s[:], recs[:, :, 0])
            mark_segments(nc, "l0m", g, src_s, order.keep, order.keep_back, order.full, order.full_back)
            node_ends(nc, "l0e", g, order, g.count_src[:], start[:], False)
            si = q.sb("si", [P, HEADS, NC])
            spread_scalars(nc, "l0i", g, order, row[:, :, 0:4], HEADS, g.scores0, src_s[:, 0:1], g.spread_s, [si[:, k, :] for k in range(HEADS)])
            mx = q.sb("mx", [P, HEADS, NC])
            heads = range(HEADS)
            segment_total(nc, "l0x", g, order, [recs[:, :, 1 + k] for k in heads], [mx[:, k, :] for k in heads], ALU.max)
            both = q.sb("both", [P, NC, 8])
            vs, asked, made = q.sem("vs"), q.sem("asked"), q.sem("made")
            with q.block() as block:
                @block.vector
                def _(eng):
                    v = nc.vector
                    chain = Chain(eng, vs)
                    for k in heads:
                        e, m = both[:, :, k], both[:, :, 4 + k]
                        t = mx[:, k, :]
                        chain(v.tensor_tensor(m, t, si[:, k, :], ALU.add))
                        chain(v.tensor_scalar(t, m, 0.2, None, ALU.mult))
                        chain(v.tensor_tensor(m, m, t, ALU.max))
                        chain(v.tensor_tensor(e, recs[:, :, 1 + k], si[:, k, :], ALU.add))
                        chain(v.tensor_scalar(t, e, 0.2, None, ALU.mult))
                        chain(v.tensor_tensor(e, e, t, ALU.max))
                        v.tensor_tensor(si[:, k, :], e, m, ALU.subtract).then_inc(asked, 1)

                @block.scalar
                def _(act):
                    for k in heads:
                        act.wait_ge(asked, k + 1)
                        nc.scalar.activation(mx[:, k, :], si[:, k, :], ACT.Exp).then_inc(made, 1)
            segment_scan(nc, "l0u", g, [mx[:, k, :] for k in heads], [si[:, k, :] for k in heads], order.keep[:], order.full, ALU.add)
            with q.block() as block:
                @block.vector
                def _(eng):
                    for k in heads:
                        nc.vector.tensor_copy(both[:, :, k], si[:, k, :])
            store_rows(nc, "l0st", [(g.stats.rearrange("(p j) w -> p j w", j=NC), both[:])])
            nodes = q.sb("nodes", [P, NB, 8])
            gather_at_nodes(nc, "l0g", g.stats, order.end_i, nodes, 8)
            with q.block() as block:
                @block.vector
                def _(eng):
                    v = nc.vector
                    chain = Chain(eng, vs)
                    chain.n = 6 * HEADS
                    v.tensor_copy(row[:, :, 4:8], nodes[:, :, 4:8])
                    v.memset(row[:, :, 12:16], 0.0)
                    chain(v.tensor_scalar(nodes[:, :, 0:4], nodes[:, :, 0:4], 1e-16, None, ALU.add))
                    chain(v.reciprocal(row[:, :, 8:12], nodes[:, :, 0:4]))
        store_rows(nc, "l0t", [(by_nodes(g.table0)[:, :, 0:D], xl[:]), (by_nodes(g.table0)[:, :, D:ROW0], row[:])])
        sum_messages(nc, "l0z", g, O.dst, g.table0, ROW0, g.src, Attended0(sj_d))
        with Space(nc, "l0f") as q:
            agg = q.sb("agg", [P, NB, D])
            finish_sum(nc, "l0y", g, O.dst, agg)
            none = q.sb("none", [P, NB])
            vs = q.sem("vs")
            with q.block() as block:
                @block.vector
                def _(eng):
                    v = nc.vector
                    chain = Chain(eng, vs)
                    chain(v.tensor_scalar(none[:], O.dst.some[:], -1.0, 1.0, ALU.mult, ALU.add))
                    v.tensor_tensor(g.x[:], g.x[:], agg[:], ALU.add)
                    chain(v.tensor_tensor(xl[:], xl[:], bc_last(none[:], D), ALU.mult))
                    chain(v.tensor_tensor(g.x[:], g.x[:], xl[:], ALU.add))
            layernorm(nc, "l0n", g.x[:], agg[:], g.eps[:])


def layer1(nc, g, O, a):
    store_rows(nc, "l1t", [(by_nodes(g.table1), g.x[:])])
    sum_messages(nc, "l1z", g, O.dst, g.table1, D, g.src, Weighed(g.weight))
    with Space(nc, "l1f") as s:
        agg = s.sb("agg", [P, NB, D])
        finish_sum(nc, "l1y", g, O.dst, agg)
        w1, w2 = s.sb("w1", [P, D]), s.sb("w2", [P, D])
        b1, b2 = s.sb("b1", [P, 1]), s.sb("b2", [P, D])
        load_weights(nc, "l1w", [(w1[:], a["L1_gnn_W1"]), (w2[:], a["L1_gnn_W2"]),
                                 (b1[:], a["L1_gnn_b1"].rearrange("(k o) -> k o", o=1)), (b2[:], row_bc(a["L1_gnn_b2"]))])
        add_nodes(nc, "l1a", agg[:], g.x[:])
        tp = [s.ps(f"tp{h}", [P, P]) for h in range(2)]
        ph = [s.ps(f"ph{h}", [P, P]) for h in range(2)]
        py = [s.ps(f"py{h}", [P, P]) for h in range(2)]
        oT, hT, y = s.sb("oT", [P, 2, P]), s.sb("hT", [P, 2, P]), s.sb("y", [P, 2, P])
        s.fed = s.sb("fed", [P, 2, P])
        t, v = nc.tensor, nc.vector

        def residual(chain, b, h):
            chain(v.tensor_tensor(y[:, h], py[h][:], b2[:], ALU.add))
            return v.tensor_tensor(xcol(g.x, b), xcol(g.x, b), y[:, h], ALU.add)

        node_loop(nc, s, agg, [
            (lambda b, h: t.transpose(tp[h][:], s.fed[:, h], g.ident[:]), lambda c, b, h: v.tensor_copy(oT[:, h], tp[h][:]), 0),
            (lambda b, h: t.matmul(ph[h][:], w1[:], oT[:, h], start=True, stop=True),
             lambda c, b, h: v.tensor_scalar(hT[:, h], ph[h][:], b1[:, 0:1], 0.0, ALU.add, ALU.max), 0),
            (lambda b, h: t.matmul(py[h][:], hT[:, h], w2[:], start=True, stop=True), residual, 1),
        ])
        layernorm(nc, "l1n", g.x[:], agg[:], g.eps[:])


def relation_tables(nc, name, g, a, wr, krv):
    with Space(nc, name) as s:
        wk2, wk3, kb = s.sb("wk2", [P, D]), s.sb("wk3", [P, D]), s.sb("kb", [P, 1])
        ids, rows = s.sb("ids", [RULES, 1], I32), s.sb("rows", [RULES, D])
        hr, rT = s.sb("hr", [P, TYPES]), s.sb("rT", [P, RULES])
        p1, p2, p3 = s.ps("p1", [P, RULES]), s.ps("p2", [P, TYPES]), s.ps("p3", [P, RULES])
        ld, got, vs, m1, a1, m2 = (s.sem(n) for n in ("ld", "got", "vs", "m1", "a1", "m2"))
        with s.block() as block:
            @block.sync
            def _(sp):
                sp.dma_start(wk2[:], a["L2_gnn_Wk_w"][D:2 * D, :]).then_inc(ld, 16)
                sp.dma_start(wk3[:], a["L2_gnn_Wk_w"][2 * D:3 * D, :]).then_inc(ld, 16)
                sp.dma_start(kb[:], a["L2_gnn_Wk_b"].rearrange("(k o) -> k o", o=1)).then_inc(ld, 16)
                sp.dma_start(ids[:], a["L2_gnn_rule_ids"].rearrange("(k o) -> k o", o=1)).then_inc(ld, 16)

            @block.gpsimd
            def _(pool):
                pool.wait_ge(ld, 64)
                nc.gpsimd.indirect_dma_start(out=rows[:], out_offset=None, in_=a["L2_gnn_rule_emb"],
                                             in_offset=bass.IndirectOffsetOnAxis(ap=ids[:, 0:1], axis=0)).then_inc(got, 16)
                pool.wait_ge(got, 16)

            @block.vector
            def _(eng):
                v = nc.vector
                chain = Chain(eng, vs)
                chain(v.tensor_reduce(hr[:], wr, AX, ALU.add))
                chain(v.tensor_scalar(hr[:], hr[:], 1.0 / D, None, ALU.mult))
                eng.wait_ge(m1, 1)
                v.tensor_copy(rT[:], p1[:]).then_inc(a1, 1)
                eng.wait_ge(m2, 1)
                v.tensor_scalar(krv[:, 0:TYPES], p2[:], kb[:, 0:1], None, ALU.add)
                v.tensor_copy(krv[:, TYPES:TYPES + RULES], p3[:])

            @block.tensor
            def _(pe):
                pe.wait_ge(got, 16)
                nc.tensor.transpose(p1[:], rows[:], g.ident[0:RULES, 0:RULES]).then_inc(m1, 1)
                pe.wait_ge(ld, 64)
                pe.wait_ge(a1, 1)
                nc.tensor.matmul(p2[:], wk2[:], hr[:], start=True, stop=True)
                nc.tensor.matmul(p3[:], wk3[:], rT[:], start=True, stop=True).then_inc(m2, 1)


def scores_and_projections(nc, name, g, order, base, qv, xT, wr):
    banks, wide = 8, TYPES * D // 8
    assert STEPS == NB - 1
    with Space(nc, name) as s:
        krow = s.sb("krow", [P, 2, U, D])
        zrow = s.sb("zrow", [P, 2, U, QROW])
        qrow = s.sb("qrow", [P, 2, U, QROW])
        prod = s.sb("prod", [P, U, D])
        pick = s.sb("pick", [P, U, TYPES])
        part = s.sb("part", [P, 2, U])
        idx = s.sb("idx", [P, 2, U], I32)
        first = s.sb("first", [P, 1], I32)
        fed = s.sb("fed", [P, P])
        proj = s.sb("proj", [P, TYPES * D])
        bank = [s.ps(f"bank{k}", [P, wide]) for k in range(banks)]
        vs, fi, fg = s.sem("vs"), s.sem("fi"), s.sem("fg")
        feed, multiplied, copied = s.sem("feed"), s.sem("multiplied"), s.sem("copied")
        stored = [s.sem(f"stored{h}") for h in range(2)]
        idx_ready, got, zgot, used = ([s.sem(f"{n}{h}") for h in range(2)] for n in ("idx", "got", "zgot", "used"))
        with s.block() as block:
            @block.vector
            def _(eng):
                v = nc.vector
                chain = Chain(eng, vs)
                chain(v.tensor_copy(first[:], g.dst[:, 0:1]))
                for h in range(2):
                    v.tensor_copy(idx[:, h], g.src[:, U * h:U * h + U]).then_inc(idx_ready[h], 1)
                v.tensor_copy(part[:, 0, 0:1], g.dst[:, 0:1]).then_inc(fi, 1)
                eng.wait_ge(fg, 16)
                with eng.Fori(0, STEPS) as i:
                    chain.loop(i, 2 * (2 * U + 6))
                    for h in range(2):
                        c = bass.ds(i * 16 + 8 * h, U)
                        hold(eng, zgot[h], i * 16 + 16)
                        for u in range(U):
                            for f in range(2):
                                if u:
                                    chain.until(1)
                                w = slice(f * QROW // 2, (f + 1) * QROW // 2)
                                prev = qrow[:, h, u - 1, w] if u else qrow[:, 1 - h, U - 1, w]
                                chain.add(v.scalar_tensor_tensor(qrow[:, h, u, w], prev, order.keep[:, bass.ds(i * 16 + 8 * h + u, 1)],
                                                                 zrow[:, h, u, w], ALU.mult, ALU.add))
                        chain.until()
                        hold(eng, got[h], i * (16 * U) + 16 * U)
                        chain.add(v.tensor_tensor(prod[:], krow[:, h], qrow[:, h, :, 0:D], ALU.mult))
                        chain.add(v.tensor_tensor(pick[:], bc_mid(g.iota[:, 0:TYPES], U), bc_last(g.type[:, c], TYPES), ALU.is_equal))
                        chain(v.tensor_copy(qv[:, :, c].rearrange("p a j -> p j a"), qrow[:, h, :, D + TYPES:QROW]))
                        chain.add(v.tensor_reduce(part[:, 0], prod[:], AX, ALU.add))
                        chain(v.tensor_tensor(pick[:], pick[:], qrow[:, h, :, D:D + TYPES], ALU.mult))
                        chain(v.tensor_reduce(part[:, 1], pick[:], AX, ALU.add))
                        v.tensor_tensor(base[:, c], part[:, 0], part[:, 1], ALU.add).then_inc(used[h], 1)
                        hold(eng, used[h], i + 1)
                        v.tensor_copy(idx[:, h], g.src[:, bass.ds(i * 16 + 16 + 8 * h, U)]).then_inc(idx_ready[h], 1)

            @block.tensor
            def _(pe):
                def column():
                    for k in range(banks):
                        nc.tensor.matmul(bank[k][:], fed[:], wr[:, k * wide:(k + 1) * wide], start=True, stop=True).then_inc(multiplied, 1)

                with pe.Fori(0, STEPS) as i:
                    hold(pe, feed, i + 1)
                    column()
                pe.wait_ge(feed, NB)
                column()

            @block.scalar
            def _(act):
                table = g.proj.rearrange("(p b r) f -> p (b r f)", b=NB, r=TYPES)
                part_wide = TYPES * D // 2
                for h in range(2):
                    act.sem_inc(stored[h], 16)
                nc.scalar.copy(fed[:], xT[:, 0, :]).then_inc(feed, 1)
                with act.Fori(0, STEPS) as i:
                    for h in range(2):
                        hold(act, stored[h], i * 16 + 16)
                        for k in range(4 * h, 4 * h + 4):
                            hold(act, multiplied, i * 8 + (k + 1))
                            nc.scalar.copy(proj[:, k * wide:(k + 1) * wide], bank[k][:]).then_inc(copied, 1)
                        hold(act, copied, i * 8 + (4 * h + 4))
                        act.dma_start(table[:, bass.ds(i * (TYPES * D) + h * part_wide, part_wide)],
                                      proj[:, h * part_wide:(h + 1) * part_wide]).then_inc(stored[h], 16)
                    nc.scalar.copy(fed[:], xcol(xT, i + 1)).then_inc(feed, 1)
                for h in range(2):
                    act.wait_ge(stored[h], 16 * NB)
                    for k in range(4 * h, 4 * h + 4):
                        act.wait_ge(multiplied, 8 * (NB - 1) + k + 1)
                        nc.scalar.copy(proj[:, k * wide:(k + 1) * wide], bank[k][:]).then_inc(copied, 1)
                    act.wait_ge(copied, 8 * (NB - 1) + 4 * h + 4)
                    lo = (NB - 1) * TYPES * D + h * part_wide
                    act.dma_start(table[:, lo:lo + part_wide], proj[:, h * part_wide:(h + 1) * part_wide]).then_inc(stored[h], 16)
                for h in range(2):
                    act.wait_ge(stored[h], 16 * (NB + 1))

            @block.gpsimd
            def _(pool):
                pool.wait_ge(fi, 1)
                nc.gpsimd.indirect_dma_start(out=qrow[:, 1, U - 1, :], out_offset=None, in_=g.table_q,
                                             in_offset=bass.IndirectOffsetOnAxis(ap=first[:, 0:1], axis=0)).then_inc(fg, 16)
                with pool.Fori(0, STEPS) as i:
                    for h in range(2):
                        hold(pool, idx_ready[h], i + 1)
                        for u in range(U):
                            nc.gpsimd.indirect_dma_start(out=krow[:, h, u, :], out_offset=None, in_=g.table_k,
                                                         in_offset=bass.IndirectOffsetOnAxis(ap=idx[:, h, u:u + 1], axis=0)).then_inc(got[h], 16)

            @block.sync
            def _(sp):
                z = g.spread_q[0:EP, :].rearrange("(p j) w -> p (j w)", j=NC)
                with sp.Fori(0, STEPS) as i:
                    for h in range(2):
                        hold(sp, idx_ready[h], i + 1)
                        sp.dma_start(zrow[:, h].rearrange("p u w -> p (u w)"),
                                     z[:, bass.ds(i * (2 * U * QROW) + h * U * QROW, U * QROW)]).then_inc(zgot[h], 16)


def layer2(nc, g, O, a):
    with Space(nc, "l2") as s:
        ready0 = s.sem("ready0")
        base, qv = s.sb("base", [P, NC]), s.sb("qv", [P, RULES, NC])
        front = Space(nc, "l2o").__enter__()
        xT = front.sb("xT", [P, NB, D])
        wr = front.sb("wr", [P, TYPES, D])
        with Space(nc, "l2a") as q:
            qn, kn = q.sb("qn", [P, NB, QROW]), q.sb("kn", [P, NB, D])
            wq, wk1, bq, bqc = q.sb("wq", [P, D]), q.sb("wk1", [P, D]), q.sb("bq", [P, D]), q.sb("bqc", [P, 1])
            krv = q.sb("krv", [P, TYPES + RULES])
            load_weights(nc, "l2w", [(wr[:], a["L2_gnn_W_r"].rearrange("r k o -> k r o")), (wq[:], a["L2_gnn_Wq_w"]),
                                     (wk1[:], a["L2_gnn_Wk_w"][0:D, :]), (bq[:], row_bc(a["L2_gnn_Wq_b"])),
                                     (bqc[:], a["L2_gnn_Wq_b"].rearrange("(k o) -> k o", o=1))])
            relation_tables(nc, "l2r", g, a, wr[:], krv)
            with Space(nc, "l2n") as t_:
                tp = [t_.ps(f"tp{h}", [P, P]) for h in range(2)]
                qk = [t_.ps(f"qk{h}", [P, 2, P]) for h in range(2)]
                pq = [t_.ps(f"pq{h}", [P, P]) for h in range(2)]
                pr = [t_.ps(f"pr{h}", [P, TYPES + RULES]) for h in range(2)]
                qT, xS = t_.sb("qT", [P, 2, P]), t_.sb("xS", [P, 2, P])
                t_.fed = t_.sb("fed", [P, 2, P])
                t, v = nc.tensor, nc.vector

                def both(b, h):
                    t.matmul(qk[h][:, 0], xS[:, h], wq[:], start=True, stop=True)
                    return t.matmul(qk[h][:, 1], xS[:, h], wk1[:], start=True, stop=True)

                def take(c, b, h):
                    v.tensor_copy(xcol(kn, b), qk[h][:, 1])
                    return v.tensor_tensor(qn[:, bass.ds(b, 1), 0:D].rearrange("p o f -> p (o f)"), qk[h][:, 0], bq[:], ALU.add)

                def keep_xT(c, b, h):
                    v.tensor_copy(xcol(xT, b), tp[h][:])
                    return v.tensor_copy(xS[:, h], tp[h][:])

                node_loop(nc, t_, g.x, [
                    (lambda b, h: t.transpose(tp[h][:], t_.fed[:, h], g.ident[:]), keep_xT, 0),
                    (both, take, 0),
                    (lambda b, h: t.matmul(pq[h][:], wq[:], xS[:, h], start=True, stop=True),
                     lambda c, b, h: v.tensor_scalar(qT[:, h], pq[h][:], bqc[:, 0:1], None, ALU.add), 0),
                    (lambda b, h: t.matmul(pr[h][:], qT[:, h], krv[:], start=True, stop=True),
                     lambda c, b, h: v.tensor_copy(qn[:, bass.ds(b, 1), D:QROW].rearrange("p o f -> p (o f)"), pr[h][:]), 0),
                ])
            store_rows(nc, "l2t", [(by_nodes(g.table_k), kn[:]), (by_nodes(g.table_q), qn[:])])
            with q.block() as block:
                sent = q.sem("sent")

                @block.gpsimd
                def _(pool):
                    for b in range(NB):
                        nc.gpsimd.indirect_dma_start(out=g.spread_q, out_offset=bass.IndirectOffsetOnAxis(ap=O.dst.start_i[:, b:b + 1], axis=0),
                                                     in_=qn[:, b, :], in_offset=None).then_inc(sent, 16)
                    pool.wait_ge(sent, 16 * NB)
        scores_and_projections(nc, "l2s", g, O.dst, base, qv, xT, wr[:].rearrange("p r o -> p (r o)"))
        front.__exit__(None, None, None)
        index, attn = s.sb("index", [P, NC + 16]), s.sb("attn", [P, NC])
        with Space(nc, "l2b") as q:
            key, mx = q.sb("key", [P, NC]), q.sb("mx", [P, NC])
            ex, tot, tmp = q.sb("ex", [P, RULES, NC]), q.sb("tot", [P, RULES, NC]), q.sb("tmp", [P, NC])
            order = Order(q, "ty")
            with q.block() as block:
                @block.vector
                def _(eng):
                    v = nc.vector
                    v.memset(index[:], 0.0).then_inc(ready0, 1)
                    v.scalar_tensor_tensor(key[:], g.dst[:, 0:NC], float(TYPES), g.type[:], ALU.mult, ALU.add)
                    eng.wait_ge(ready0, 1)
                    v.scalar_tensor_tensor(index[:, 0:NC], g.src[:, 0:NC], float(TYPES), g.type[:], ALU.mult, ALU.add)
            mark_segments(nc, "l2m", g, key, order.keep, order.keep_back, order.full, order.full_back)
            segment_total(nc, "l2x", g, order, [base[:]], [mx[:]], ALU.max)
            vs, asked, made = q.sem("vs"), q.sem("asked"), q.sem("made")
            scale = float(D) ** -0.5
            with q.block() as block:
                @block.vector
                def _(eng):
                    v = nc.vector
                    chain = Chain(eng, vs)
                    for k in range(RULES):
                        chain(v.tensor_tensor(tmp[:], mx[:], qv[:, k, :], ALU.add))
                        chain(v.tensor_scalar(tmp[:], tmp[:], scale, None, ALU.mult))
                        chain(v.tensor_tensor(tot[:, k, :], base[:], qv[:, k, :], ALU.add))
                        v.scalar_tensor_tensor(ex[:, k, :], tot[:, k, :], scale, tmp[:], ALU.mult, ALU.subtract).then_inc(asked, 1)
                        eng.wait_ge(asked, k + 1)

                @block.scalar
                def _(act):
                    for k in range(RULES):
                        act.wait_ge(asked, k + 1)
                        nc.scalar.activation(ex[:, k, :], ex[:, k, :], ACT.Exp).then_inc(made, 1)
            rules = range(RULES)
            segment_total(nc, "l2u", g, order, [ex[:, k, :] for k in rules], [tot[:, k, :] for k in rules], ALU.add)
            v2 = q.sem("v2")
            with q.block() as block:
                @block.vector
                def _(eng):
                    v = nc.vector
                    chain = Chain(eng, v2)
                    chain(v.reciprocal(tot[:], tot[:]))
                    chain(v.tensor_tensor(ex[:], ex[:], tot[:], ALU.mult))
                    chain(v.tensor_tensor(tmp[:], ex[:, 0, :], ex[:, 1, :], ALU.add))
                    chain(v.tensor_tensor(tmp[:], tmp[:], ex[:, 2, :], ALU.add))
                    chain(v.tensor_tensor(tmp[:], tmp[:], ex[:, 3, :], ALU.add))
                    v.tensor_scalar(attn[:], tmp[:], 1.0 / RULES, None, ALU.mult)
        sum_messages(nc, "l2z", g, O.dst, g.proj, D, index, Weighed(attn))
    with Space(nc, "l2f") as s:
        agg, sq = s.sb("agg", [P, NB, D]), s.sb("sq", [P, NB, D])
        finish_sum(nc, "l2y", g, O.dst, agg)
        bias, gamma, beta = (s.sb(n, [P, D]) for n in ("bias", "gamma", "beta"))
        load_weights(nc, "l2v", [(bias[:], row_bc(a["L2_gnn_bias"])), (gamma[:], row_bc(a["L2_gnn_ln_gamma"])),
                                 (beta[:], row_bc(a["L2_gnn_ln_beta"]))])
        add_nodes(nc, "l2c", agg[:], bc_mid(bias[:], NB))
        layernorm(nc, "l2d", agg[:], sq[:], g.eps[:], gamma[:], beta[:], relu=True)
        add_nodes(nc, "l2e", g.x[:], agg[:])
        layernorm(nc, "l2g", g.x[:], sq[:], g.eps[:])


def layer3(nc, g, O, a):
    with Space(nc, "l3") as s:
        hn = s.sb("hn", [P, NB, D])
        sn = s.sb("sn", [P, NB, 4])
        stat = s.sb("stat", [P, NB, 4])
        ends = s.sb("ends", [P, 2])
        with Space(nc, "l3a") as q:
            w, att = q.sb("w", [P, D]), q.sb("att", [P, 2])
            scores = q.sb("scores", [P, NB, 2])
            load_weights(nc, "l3w", [(w[:], a["L3_gnn_W"]), (att[:, 0:1], a["L3_gnn_a_src"].rearrange("(k o) -> k o", o=1)),
                                     (att[:, 1:2], a["L3_gnn_a_dst"].rearrange("(k o) -> k o", o=1))])
            project_and_score(nc, "l3p", g, w[:], None, att[:], 2, hn, scores)
            with q.block() as block:
                @block.vector
                def _(eng):
                    nc.vector.tensor_copy(sn[:, :, 0:2], scores[:])
                    nc.vector.memset(sn[:, :, 2:4], 0.0)
        store_rows(nc, "l3t", [(by_nodes(g.table3)[:, :, 0:D], hn[:]), (by_nodes(g.table3)[:, :, D:D + 4], sn[:])])
        with Space(nc, "l3b") as q:
            sd = q.sb("sd", [P, NC])
            both = q.sb("both", [P, NC, 4])
            spread_scalars(nc, "l3d", g, O.dst, sn[:], 4, g.scores0, g.dst[:, 0:1], g.spread_3, [None, sd[:]])
            with q.block() as block:
                @block.vector
                def _(eng):
                    nc.vector.memset(both[:, :, 2:4], 0.0)
            sum_messages(nc, "l3z", g, O.dst, g.table3, D + 4, g.src, Online3(sd, both, both))
            with q.block() as block:
                @block.vector
                def _(eng):
                    nc.vector.tensor_copy(ends[:], both[:, NC - 1, 0:2])
            store_rows(nc, "l3s", [(g.stats4.rearrange("(p j) w -> p j w", j=NC), both[:])])
            gather_at_nodes(nc, "l3h", g.stats4, O.dst.end_i, stat, 4)
        agg = s.sb("agg", [P, NB, D])
        carried = s.sb("carried", [P, NB, D + 2])
        finish_sum(nc, "l3y", g, O.dst, agg, online=(ends[:, 0:1], ends[:, 1:2], carried))
        bias = s.sb("bias", [P, D])
        load_weights(nc, "l3v", [(bias[:], row_bc(a["L3_gnn_bias"]))])
        own, most, t, fe, fc, fs = (s.sb(n, [P, NB]) for n in ("own", "most", "t", "fe", "fc", "fs"))
        vs, asked, made = s.sem("vs"), s.sem("asked"), s.sem("made")
        with s.block() as block:
            @block.vector
            def _(eng):
                v = nc.vector
                chain = Chain(eng, vs)

                def known(out, value, there):
                    chain(v.tensor_tensor(out, value, there, ALU.mult))
                    chain(v.tensor_scalar(t[:], there, BIG, -BIG, ALU.mult, ALU.add))
                    chain(v.tensor_tensor(out, out, t[:], ALU.add))

                chain(v.tensor_tensor(own[:], sn[:, :, 0], sn[:, :, 1], ALU.add))
                chain(v.scalar_tensor_tensor(own[:], own[:], 0.2, own[:], ALU.mult, ALU.max))
                known(fe[:], stat[:, :, 0], O.dst.some[:])
                known(fc[:], carried[:, :, D + 1], O.dst.span[:])
                chain(v.tensor_tensor(most[:], fe[:], own[:], ALU.max))
                chain(v.tensor_tensor(most[:], most[:], fc[:], ALU.max))
                v.tensor_tensor(fe[:], fe[:], most[:], ALU.subtract)
                v.tensor_tensor(fc[:], fc[:], most[:], ALU.subtract)
                v.tensor_tensor(fs[:], own[:], most[:], ALU.subtract).then_inc(asked, 1)
                eng.wait_ge(made, 3)
                chain(v.tensor_tensor(own[:], stat[:, :, 1], fe[:], ALU.mult))
                chain(v.tensor_tensor(t[:], carried[:, :, D], fc[:], ALU.mult))
                chain(v.tensor_tensor(t[:], t[:], own[:], ALU.add))
                chain(v.tensor_tensor(t[:], t[:], fs[:], ALU.add))
                chain(v.reciprocal(t[:], t[:]))
                v.tensor_tensor(fe[:], fe[:], t[:], ALU.mult)
                v.tensor_tensor(fc[:], fc[:], t[:], ALU.mult)
                chain(v.tensor_tensor(fs[:], fs[:], t[:], ALU.mult))
                v.tensor_tensor(agg[:], agg[:], bc_last(fe[:], D), ALU.mult)
                v.tensor_tensor(carried[:, :, 0:D], carried[:, :, 0:D], bc_last(fc[:], D), ALU.mult)
                chain(v.tensor_tensor(hn[:], hn[:], bc_last(fs[:], D), ALU.mult))
                chain(v.tensor_tensor(agg[:], agg[:], hn[:], ALU.add))
                chain(v.tensor_tensor(agg[:], agg[:], carried[:, :, 0:D], ALU.add))
                chain(v.tensor_tensor(agg[:], agg[:], bc_mid(bias[:], NB), ALU.add))
                chain(v.scalar_tensor_tensor(agg[:], agg[:], 0.2, agg[:], ALU.mult, ALU.max))
                v.tensor_tensor(g.x[:], g.x[:], agg[:], ALU.add)

            @block.scalar
            def _(act):
                act.wait_ge(asked, 1)
                nc.scalar.activation(fe[:], fe[:], ACT.Exp).then_inc(made, 1)
                nc.scalar.activation(fc[:], fc[:], ACT.Exp).then_inc(made, 1)
                nc.scalar.activation(fs[:], fs[:], ACT.Exp).then_inc(made, 1)
        layernorm(nc, "l3n", g.x[:], agg[:], g.eps[:])


class Shared:
    pass


def kernel_body(nc, a, out, layers=4):
    with Space(nc, "g") as s:
        g, O = Shared(), Shared()

        def dram(name, shape):
            return nc.dram_tensor(name, shape, F32, kind="Internal").ap()

        g.rec_type, g.rec_dst, g.by_src = dram("rec_type", (EP, 4)), dram("rec_dst", (EP, 4)), dram("by_src", (EP, 8))
        g.spread_q, g.spread_s = dram("spread_q", (EP + NP, QROW)), dram("spread_s", (EP + NP, 4))
        g.spread_0, g.spread_3 = dram("spread_0", (EP + NP, 4)), dram("spread_3", (EP + NP, 4))
        g.scores0, g.stats, g.stats4 = dram("scores0", (NP, 4)), dram("stats", (EP, 8)), dram("stats4", (EP, 4))
        g.table0, g.table1 = dram("table0", (NP, ROW0)), dram("table1", (NP, D))
        g.table3 = dram("table3", (NP, D + 4))
        g.table_q, g.table_k, g.proj = dram("table_q", (NP, QROW)), dram("table_k", (NP, D)), dram("proj", (NP * TYPES, D))
        g.prefix, g.carry_row = dram("prefix", (EP, D)), dram("carry_row", (NP,))
        g.x = s.sb("x", [P, NB, D])
        g.zmat, g.ones, g.iota, g.ident, g.after = (s.sb(n, [P, P]) for n in ("zmat", "ones", "iota", "ident", "after"))
        g.identb = s.sb("identb", [P, P], BF16)
        g.part, g.eps, g.tail = s.sb("part", [P, 1]), s.sb("eps", [P, 1]), s.sb("tail", [P, D])
        g.src, g.dst = s.sb("src", [P, NC + 16]), s.sb("dst", [P, NC + 16])
        g.type, g.weight = s.sb("type", [P, NC]), s.sb("weight", [P, NC])
        g.count_src = s.sb("count_src", [P, NB])
        O.dst = Order(s, "do")
        with Space(nc, "prep") as q:
            g.rec = q.sb("rec", [P, NC, 4])
            g.zero = q.sb("zero", [P, U * QROW])
            count, start, count_dst = (q.sb(n, [P, NB]) for n in ("count", "start", "count_dst"))
            key = q.sb("key", [P, NC])
            load_inputs(nc, g, a["x"], a["src"], a["dst"], a["edge_type_32"], a["edge_weight"])
            with q.block() as block:
                @block.vector
                def _(eng):
                    nc.vector.memset(g.eps[:], 1e-5)
                    nc.vector.tensor_scalar(key[:], g.rec[:, :, 2], float(NB), None, ALU.mult)
            sort_by(nc, "st", g, key[:], g.rec, 4, g.rec_type, True, count[:], start[:],
                    types=True, clear=g.spread_q, ahead=(g.rec[:, :, 1], count_dst[:]))
            reload_rows(nc, "rt", g.rec[:], g.rec_type, 4)
            sort_by(nc, "sd", g, g.rec[:, :, 1], g.rec, 4, g.rec_dst, False, count_dst[:], start[:],
                    ahead=(g.rec[:, :, 0], g.count_src[:]))
            reload_rows(nc, "rd", g.rec[:], g.rec_dst, 4)
            vs = q.sem("vs")
            with q.block() as block:
                @block.vector
                def _(eng):
                    v = nc.vector
                    v.memset(g.src[:], 0.0)
                    v.memset(g.dst[:], 0.0).then_inc(vs, 1)
                    eng.wait_ge(vs, 1)
                    v.tensor_copy(g.src[:, 0:NC], g.rec[:, :, 0])
                    v.tensor_copy(g.dst[:, 0:NC], g.rec[:, :, 1])
                    v.tensor_copy(g.type[:], g.rec[:, :, 2])
                    v.tensor_copy(g.weight[:], g.rec[:, :, 3])
            mark_segments(nc, "dm", g, g.dst, O.dst.keep, O.dst.keep_back, O.dst.full, O.dst.full_back)
            node_ends(nc, "de", g, O.dst, count_dst[:], start[:], True)
        for layer in (layer0, layer1, layer2, layer3)[:layers]:
            layer(nc, g, O, a)
        store_rows(nc, "out", [(out.rearrange("(p b) f -> p b f", b=NB), g.x[0:NREAL, :, :])])


_INS = ['x', 'src', 'dst', 'edge_type_32', 'edge_weight', 'L0_gnn_W_lin', 'L0_gnn_b_lin', 'L0_gnn_W_att', 'L0_gnn_b_att',
        'L1_gnn_W1', 'L1_gnn_b1', 'L1_gnn_W2', 'L1_gnn_b2', 'L2_gnn_W_r', 'L2_gnn_Wq_w', 'L2_gnn_Wq_b', 'L2_gnn_Wk_w',
        'L2_gnn_Wk_b', 'L2_gnn_rule_emb', 'L2_gnn_bias', 'L2_gnn_ln_gamma', 'L2_gnn_ln_beta', 'L2_gnn_rule_ids',
        'L3_gnn_W', 'L3_gnn_a_src', 'L3_gnn_a_dst', 'L3_gnn_bias']
LAYERS = 4


def kernel(**inputs):
    import numpy as _np
    import concourse.bacc as _bacc
    from concourse import mybir as _mybir
    from concourse.bass_utils import run_bass_kernel_spmd as _run

    nc = _bacc.Bacc("TRN2", target_bir_lowering=False, num_devices=1)
    arrays, args = {}, {}
    for name in _INS:
        arr = _np.ascontiguousarray(inputs[name])
        arrays[f"in_{name}_dram"] = arr
        args[name] = nc.dram_tensor(f"in_{name}_dram", arr.shape, _mybir.dt.from_np(arr.dtype), kind="ExternalInput").ap()
    out = nc.dram_tensor("out_0_dram", (N_NODES, D), F32, kind="ExternalOutput").ap()
    kernel_body(nc, args, out, LAYERS)
    r = _run(nc, [arrays], core_ids=[0])
    return r.results[0]["out_0_dram"]
```
